# Optimizing a Trainium2 kernel written in Bass

```python
import numpy as np
import jax
import jax.numpy as jnp

def _softmax(x, axis=-1):
    return jax.nn.softmax(x, axis=axis)

def _gelu(x):
    return jax.nn.gelu(x, approximate=True)

def _silu(x):
    return jax.nn.silu(x)

def _sigmoid(x):
    return jax.nn.sigmoid(x)

def _layernorm(x, axis=-1, eps=1e-05):
    m = jnp.mean(x, axis=axis, keepdims=True)
    v = jnp.var(x, axis=axis, keepdims=True)
    return (x - m) / jnp.sqrt(v + eps)

def _scatter_add(tgt, idx, src, axis=0):
    return tgt.at[idx].add(src)

def _segment_sum(src, seg, n):
    return jax.ops.segment_sum(src, seg, n)
kernel_name = 'mk_xattn_ffn_d1_seqx_r8_773ff0'

def setup_inputs(seed: int=0):
    np.random.seed(seed)
    _w = jnp.asarray

    def _rec_inputs():
        import jax
        import jax.numpy as jnp
        _rk = jax.random.key(seed)
        x = -0.0002928 + 1 * jax.random.normal(jax.random.fold_in(_rk, 1), (8, 128, 128), jnp.float32)
        _lenS = 128 - jax.random.randint(jax.random.fold_in(_rk, 7), (8,), 0, max(1, 128 // 4) + 1, jnp.int32)
        _lenS2 = 128 - jax.random.randint(jax.random.fold_in(_rk, 8), (8,), 0, max(1, 128 // 4) + 1, jnp.int32)
        _ctx_1024P = jax.random.normal(jax.random.fold_in(_rk, 11), (8, 16, 128), jnp.float32)
        _ctx_1024c = jax.random.dirichlet(jax.random.fold_in(_rk, 511), 0.3 * jnp.ones((16,), jnp.float32), (8, 128))
        _ctx_1024t = jnp.einsum('bsk,bkd->bsd', _ctx_1024c, _ctx_1024P)
        _ctx_1024t = _ctx_1024t * jax.lax.rsqrt(jnp.mean(jnp.square(_ctx_1024t)) + 1e-12) * 0.953939
        ctx_1024 = -1.39393e-06 + 0.999914 * (_ctx_1024t + 0.3 * jax.random.normal(jax.random.fold_in(_rk, 611), (8, 128, 128), jnp.float32))
        return (x, ctx_1024)
    x, ctx_1024 = _rec_inputs()

    def _L0_xattn_setup():
        import jax, jax.numpy as jnp
        import numpy as np
        D_MODEL = 128
        NUM_HEADS = 16
        D_K = D_MODEL // NUM_HEADS
        key = jax.random.key(seed)
        ks = jax.random.split(key, 11)
        B, S, D = (2, 256, D_MODEL)
        s = 1.0 / np.sqrt(D)
        return {'query': jax.random.normal(ks[0], (B, S, D), jnp.float32), 'key': jax.random.normal(ks[1], (B, S, D), jnp.float32), 'value': jax.random.normal(ks[2], (B, S, D), jnp.float32), 'Wq': jax.random.normal(ks[3], (D, D), jnp.float32) * s, 'bq': jnp.zeros((D,), jnp.float32), 'Wk': jax.random.normal(ks[4], (D, D), jnp.float32) * s, 'bk': jnp.zeros((D,), jnp.float32), 'Wv': jax.random.normal(ks[5], (D, D), jnp.float32) * s, 'bv': jnp.zeros((D,), jnp.float32), 'Wo': jax.random.normal(ks[6], (D, D), jnp.float32) * s, 'bo': jnp.zeros((D,), jnp.float32)}
    _L0_xattn_all = _L0_xattn_setup()
    _L0_xattn_in = {k: v for k, v in _L0_xattn_all.items() if k in ('Wq', 'bq', 'Wk', 'bk', 'Wv', 'bv', 'Wo', 'bo')}
    del _L0_xattn_all

    def _L0_ffn_setup():
        import jax, jax.numpy as jnp
        import numpy as np
        E = 8
        K = 2
        C = 128
        F = 256
        EPS = 1e-05
        key = jax.random.key(seed)
        ks = jax.random.split(key, 6)
        x = jax.random.normal(ks[0], (2, 128, C), dtype=jnp.float32)
        ln_gamma = 1.0 + 0.02 * jax.random.normal(ks[1], (C,), dtype=jnp.float32)
        ln_beta = 0.02 * jax.random.normal(ks[2], (C,), dtype=jnp.float32)
        gate_w = jax.random.normal(ks[3], (E, C), dtype=jnp.float32) / np.sqrt(C)
        w1 = jax.random.normal(ks[4], (E, F, C), dtype=jnp.float32) / np.sqrt(C)
        w2 = jax.random.normal(ks[5], (E, C, F), dtype=jnp.float32) / np.sqrt(F)
        return {'x': x, 'ln_gamma': ln_gamma, 'ln_beta': ln_beta, 'gate_w': gate_w, 'w1': w1, 'w2': w2}
    _L0_ffn_all = _L0_ffn_setup()
    _L0_ffn_in = {k: v for k, v in _L0_ffn_all.items() if k in ('ln_gamma', 'ln_beta', 'gate_w', 'w1', 'w2')}
    del _L0_ffn_all
    return {'x': x, 'ctx_1024': ctx_1024, 'L0_xattn_Wq': _L0_xattn_in['Wq'], 'L0_xattn_bq': _L0_xattn_in['bq'], 'L0_xattn_Wk': _L0_xattn_in['Wk'], 'L0_xattn_bk': _L0_xattn_in['bk'], 'L0_xattn_Wv': _L0_xattn_in['Wv'], 'L0_xattn_bv': _L0_xattn_in['bv'], 'L0_xattn_Wo': _L0_xattn_in['Wo'], 'L0_xattn_bo': _L0_xattn_in['bo'], 'L0_ffn_ln_gamma': _L0_ffn_in['ln_gamma'], 'L0_ffn_ln_beta': _L0_ffn_in['ln_beta'], 'L0_ffn_gate_w': _L0_ffn_in['gate_w'], 'L0_ffn_w1': _L0_ffn_in['w1'], 'L0_ffn_w2': _L0_ffn_in['w2']}

def reference(x, ctx_1024, L0_xattn_Wq, L0_xattn_bq, L0_xattn_Wk, L0_xattn_bk, L0_xattn_Wv, L0_xattn_bv, L0_xattn_Wo, L0_xattn_bo, L0_ffn_ln_gamma, L0_ffn_ln_beta, L0_ffn_gate_w, L0_ffn_w1, L0_ffn_w2):
    import jax
    import jax.numpy as jnp

    def _L0_xattn_ref(query, key, value, Wq, bq, Wk, bk, Wv, bv, Wo, bo):
        import jax, jax.numpy as jnp
        import numpy as np
        D_MODEL = 128
        NUM_HEADS = 16
        D_K = D_MODEL // NUM_HEADS
        B, S, D = query.shape
        H, Dk = (NUM_HEADS, D_K)
        q = (query @ Wq + bq).reshape(B, S, H, Dk).transpose(0, 2, 1, 3)
        k = (key @ Wk + bk).reshape(B, S, H, Dk).transpose(0, 2, 1, 3)
        v = (value @ Wv + bv).reshape(B, S, H, Dk).transpose(0, 2, 1, 3)
        scores = jnp.einsum('bhqd,bhkd->bhqk', q, k) / jnp.sqrt(jnp.float32(Dk))
        attn = jax.nn.softmax(scores, axis=-1)
        out = jnp.einsum('bhqk,bhkd->bhqd', attn, v)
        out = out.transpose(0, 2, 1, 3).reshape(B, S, D)
        return out @ Wo + bo

    def _L0_ffn_ref(x, ln_gamma, ln_beta, gate_w, w1, w2):
        import jax, jax.numpy as jnp
        import numpy as np
        E = 8
        K = 2
        C = 128
        F = 256
        EPS = 1e-05
        B, T, Cc = x.shape
        xf = x.reshape(-1, Cc)
        mu = jnp.mean(xf, axis=-1, keepdims=True)
        var = jnp.var(xf, axis=-1, keepdims=True)
        rn = (xf - mu) * jax.lax.rsqrt(var + EPS) * ln_gamma + ln_beta
        logits = rn @ gate_w.T
        probs = jax.nn.softmax(logits, axis=-1)
        rw, sel = jax.lax.top_k(probs, K)
        comb = jnp.sum(jax.nn.one_hot(sel, E, dtype=xf.dtype) * rw[..., None], axis=1)
        h = jax.nn.gelu(jnp.einsum('nc,efc->enf', xf, w1), approximate=False)
        y = jnp.einsum('enf,ecf->enc', h, w2)
        out = jnp.einsum('enc,ne->nc', y, comb)
        return out.reshape(B, T, Cc)
    x = x + _L0_xattn_ref(_layernorm(x, axis=-1), ctx_1024, ctx_1024, L0_xattn_Wq, L0_xattn_bq, L0_xattn_Wk, L0_xattn_bk, L0_xattn_Wv, L0_xattn_bv, L0_xattn_Wo, L0_xattn_bo)
    x = x + _L0_ffn_ref(_layernorm(x, axis=-1), L0_ffn_ln_gamma, L0_ffn_ln_beta, L0_ffn_gate_w, L0_ffn_w1, L0_ffn_w2)
    return x

_drawn_inputs = setup_inputs


def setup_inputs(seed=0):
    import zlib

    import numpy as np

    out = dict(_drawn_inputs(seed))
    spreads = {'L0_xattn_bq': (0.0, 0.1),
     'L0_xattn_bk': (0.0, 2.0),
     'L0_xattn_bv': (0.0, 0.1),
     'L0_xattn_bo': (0.0, 0.1)}
    factors = {'L0_ffn_ln_gamma': 25.774, 'L0_ffn_ln_beta': 17.638}
    for name, (base, spread) in spreads.items():
        noise = np.random.default_rng([zlib.crc32(name.encode()), seed]).standard_normal(out[name].shape)
        drawn = base * np.exp(spread * noise) if base else spread * noise
        out[name] = jnp.asarray(drawn.astype(out[name].dtype))
    for name, factor in factors.items():
        out[name] = (out[name] * factor).astype(out[name].dtype)
    return out
```

```python
from contextlib import ExitStack

import concourse.bass as bass
from concourse import mybir

F32 = mybir.dt.float32
F32R = mybir.dt.float32r
BF16 = mybir.dt.bfloat16
I32 = mybir.dt.int32
ALU = mybir.AluOpType
ACT = mybir.ActivationFunctionType
AX_X = mybir.AxisListType.X

P = 128
B, S, D = 8, 128, 128
H, DK = 16, 8
G = H // 2
E, F = 8, 256
FH = F // P
EPS = 1e-5
SEGS = 6
K_SEG_PART = (0, 1, 2, 0, 1, 0)
Q_SEG_PART = (0, 0, 0, 1, 1, 2)
VW = DK + 1
WIN = 96
VCOLS = H * VW + WIN - VW
HALF = 4
CH = 2
UNITS = E * CH


def build(nc, x, ctxT, Wq, Wk, Wv, Wo, bq, bk, bv, bo, gamma, beta, gateT, w1T, w2T, ident, low, ones, out):
    with ExitStack() as ctx:
        def sb(name, shape, dt=F32):
            return ctx.enter_context(nc.sbuf_tensor(name, shape, dt))

        def sem(name):
            return ctx.enter_context(nc.semaphore(name))

        x_all = sb("x_all", [P, B, D])
        ctx_T = sb("ctx_T", [P, B * S])
        wq_sb, wk_sb, wv_sb, wo_sb = (sb(n, [P, D]) for n in ("wq_sb", "wk_sb", "wv_sb", "wo_sb"))
        bq_sb, bk_sb, gam_sb, bet_sb = (sb(n, [P, 1]) for n in ("bq_sb", "bk_sb", "gam_sb", "bet_sb"))
        bv_sb, bo_sb = sb("bv_sb", [P, D]), sb("bo_sb", [P, D])
        gate_sb = sb("gate_sb", [P, E])
        id_sb = sb("id_sb", [P, P])
        id_bf = sb("id_bf", [P, P], BF16)
        low_sb = sb("low_sb", [P, E, E])
        ones_mat = sb("ones_mat", [P, P])
        stats1 = sb("stats1", [P, B, 6])
        mv1 = sb("mv1", [P, B, 2])
        consts = sb("consts", [P, 2, B])
        rs1 = sb("rs1", [P, 2, B])
        xn = sb("xn", [P, B, D])
        xn_T = sb("xn_T", [P, B * S])
        k_part = sb("k_part", [P, 3, B * S], BF16)
        q_part = sb("q_part", [P, 3, B * S], BF16)
        rest = sb("rest", [P, 4, HALF * S])
        k_res = sb("k_res", [P, G, B, S], BF16)
        q_res = sb("q_res", [P, G, B, S], BF16)
        v_res = sb("v_res", [P, B, VCOLS])
        k_st = [sb(f"k_st{u}", [P, G, S], BF16) for u in range(2)]
        q_st = [sb(f"q_st{u}", [P, G, S], BF16) for u in range(2)]
        v_st = [sb(f"v_st{u}", [P, VCOLS]) for u in range(2)]
        mx = [sb(f"mx{u}", [P, 2, G]) for u in range(2)]
        nm = [sb(f"nm{u}", [P, 2, 2, G], BF16) for u in range(2)]
        nm_T = [sb(f"nm_T{u}", [4 * G, S], BF16) for u in range(2)]
        prob = [sb(f"prob{h}", [P, 2, G // 2, S]) for h in range(2)]
        rden = sb("rden", [P, 2, H // 2])
        o_n = [sb(f"o_n{u}", [P, D]) for u in range(2)]
        o_T = [sb(f"o_T{u}", [P, S]) for u in range(2)]
        stats2 = [sb(f"stats2{u}", [P, 6]) for u in range(2)]
        mv2 = [sb(f"mv2{u}", [P, 2]) for u in range(2)]
        rs2 = [sb(f"rs2{u}", [P, 2, 1]) for u in range(2)]
        xf = [sb(f"xf{u}", [P, D]) for u in range(2)]
        stats3 = sb("stats3", [P, B, 6])
        mv3 = sb("mv3", [P, B, 2])
        rs3 = sb("rs3", [P, 2, B])
        xf_hi = sb("xf_hi", [P, B * S], F32R)
        xf_lo = sb("xf_lo", [P, B * S], F32R)
        gb = sb("gb", [P, 2, E])
        g_hi, g_lo = sb("g_hi", [P, E], F32R), sb("g_lo", [P, E], F32R)
        gsum = sb("gsum", [P, 2, E])
        lg = sb("lg", [P, 4, B, E])
        lmax, lsum, lrec = sb("lmax", [P, B]), sb("lsum", [P, B]), sb("lrec", [P, B])
        pr = sb("pr", [P, B, E])
        rk = sb("rk", [P, 2, B, E, E])
        rank = sb("rank", [P, B, E])
        comb = sb("comb", [P, B, E])
        w1_raw = [sb(f"w1_raw{u}", [P, F]) for u in range(2)]
        w1_hi = [sb(f"w1_hi{u}", [P, F], F32R) for u in range(2)]
        w1_lo = [sb(f"w1_lo{u}", [P, F], F32R) for u in range(2)]
        w2_sb = [sb(f"w2_sb{u}", [P, FH, D]) for u in range(2)]
        h_sb = [sb(f"h_sb{u}", [P, FH, 512]) for u in range(2)]
        cw = [sb(f"cw{u}", [P, B]) for u in range(2)]

        ps = ctx.enter_context(nc.psum_tensor("ps", [P, 8, 512], F32))
        ps_s = ps[:, 0:2, :].rearrange("p j (g n) -> p j g n", n=S)
        ps_t = ps[:, 2:4, :].rearrange("p j (g n) -> p j g n", n=S)
        ps_o = [ps[:, 4 + h, :] for h in range(2)]
        ps_a, ps_b = ps[:, 6, :], ps[:, 7, :]
        ps_nm = ps_a[0:4 * G, 0:S // 2].bitcast(BF16)
        ps_xT = ps_a[:, 128:256]
        ps_oT, ps_op = ps_b[:, 0:128], ps_b[:, 128:256]

        in_x = [sem(f"in_x{h}") for h in range(2)]
        in_ctx, in_wk, in_wq, in_wv, in_wo = (sem(n) for n in ("in_ctx", "in_wk", "in_wq", "in_wv", "in_wo"))
        in_misc, in_id, in_kones = sem("in_misc"), sem("in_id"), sem("in_kones")
        filled_c, filled_k, filled_q, filled_v, filled_1 = sem("filled_c"), sem("filled_k"), sem("filled_q"), sem("filled_v"), sem("filled_1")
        id_ready = sem("id_ready")
        st1_done, mv1_done, rstd1_done, xn_done = sem("st1_done"), sem("mv1_done"), sem("rstd1_done"), sem("xn_done")
        pool_step = sem("pool_step")
        xnT_done, xnT_sb = sem("xnT_done"), sem("xnT_sb")
        proj_done = [sem(f"proj{n}_done") for n in range(4)]
        hi_done = [sem(f"hi{n}_done") for n in range(4)]
        rest_done = [sem(f"rest{n}_done") for n in range(4)]
        mid_done = [sem(f"mid{n}_done") for n in range(4)]
        lo_done = [sem(f"lo{n}_done") for n in range(4)]
        stack_k = [sem(f"stack_k{h}") for h in range(2)]
        stack_q = [sem(f"stack_q{h}") for h in range(2)]
        vproj_done, v_done = sem("vproj_done"), sem("v_done")
        v_in = [sem(f"v_in{u}") for u in range(2)]
        kst_done, qst_done = sem("kst_done"), sem("qst_done")
        row_in = [sem(f"row_in{u}") for u in range(2)]
        s_done, max_done, nmh_done, nm_done, nmT_done, nmT_sb = (
            sem(n) for n in ("s_done", "max_done", "nmh_done", "nm_done", "nmT_done", "nmT_sb"))
        t_done, p_done, av_done, rden_done, on_done = (
            sem(n) for n in ("t_done", "p_done", "av_done", "rden_done", "on_done"))
        oT_done, oT_sb, op_done, x1_done, st2_done, mv2_done, rstd2_done, xf_done, st3_done = (
            sem(n) for n in ("oT_done", "oT_sb", "op_done", "x1_done", "st2_done", "mv2_done", "rstd2_done",
                             "xf_done", "st3_done"))
        xT_done, xhi_done, xlo_done, xb_done = sem("xT_done"), sem("xhi_done"), sem("xlo_done"), sem("xb_done")
        gb_done, ghi_done, glo_done, gsum_mm, gsum_done = (
            sem(n) for n in ("gb_done", "ghi_done", "glo_done", "gsum_mm", "gsum_done"))
        mv3_done, rstd3_done, lg_mm, gate_step, lexp_done, comb_done = (
            sem(n) for n in ("mv3_done", "rstd3_done", "lg_mm", "gate_step", "lexp_done", "comb_done"))
        w1_in = [sem(f"w1_in{u}") for u in range(2)]
        w2_in = [sem(f"w2_in{u}") for u in range(2)]
        w1h_done, w1l_done = sem("w1h_done"), sem("w1l_done")
        f1_done, gelu_done, f2_done, cw_done, acc_done = (
            sem(n) for n in ("f1_done", "gelu_done", "f2_done", "cw_done", "acc_done"))
        out_done = sem("out_done")

        block = ctx.enter_context(nc.Block())

        def after(eng, s, n):
            if not isinstance(n, int) or n > 0:
                eng.wait_ge(s, n)

        def both(t, c):
            return 2 * t + c

        def attention_steps(step):
            def run(eng):
                for c in range(2):
                    step(0, c, c)
                with eng.Fori(1, B // 2 - 1) as t:
                    for c in range(2):
                        step(t, c, 2 + c)
                for c in range(2):
                    step(B // 2 - 1, c, B - 2 + c)
            return run


        @block.sync
        def _(sp):
            x_v = x.rearrange("b s d -> s b d")
            sp.dma_start(x_all[:, 0:HALF, :], x_v[:, 0:HALF, :]).then_inc(in_x[0], 16)
            sp.dma_start(wk_sb[:, :], Wk).then_inc(in_wk, 16)
            sp.dma_start(ctx_T[:, :], ctxT).then_inc(in_ctx, 16)
            sp.dma_start(id_sb[:, :], ident).then_inc(in_id, 16)
            sp.dma_start(bk_sb[:, :], bk).then_inc(in_wk, 16)
            sp.dma_start(wq_sb[:, :], Wq).then_inc(in_wq, 16)
            sp.dma_start(bq_sb[:, :], bq).then_inc(in_wq, 16)
            sp.dma_start(x_all[:, HALF:B, :], x_v[:, HALF:B, :]).then_inc(in_x[1], 16)

            def segments(part, res, seg_part, h, hi, rst, lo, fill, done):
                for want, (s_ready) in ((0, hi), (1, rst), (2, lo)):
                    for s in range(SEGS):
                        if seg_part[s] == want:
                            sp.wait_ge(s_ready, 1)
                            sp.wait_ge(fill, 1 + h)
                            dst = res[s:P:DK, :, HALF * h:HALF * (h + 1), :].rearrange("p g b n -> p g (b n)")
                            src = part[:, want, HALF * S * h:HALF * S * (h + 1)]
                            sp.dma_start(dst, src).then_inc(done, 16)

            segments(k_part, k_res, K_SEG_PART, 0, hi_done[0], mid_done[0], lo_done[0], filled_k, stack_k[0])
            segments(q_part, q_res, Q_SEG_PART, 0, hi_done[1], mid_done[1], lo_done[1], filled_q, stack_q[0])

            def load_v(t, c):
                u = c % 2
                after(sp, av_done, 2 * both(t, c) - 2)
                sp.dma_start(v_st[u][:, :], v_res[:, both(t, c), :]).then_inc(v_in[u], 16)

            def rows(t, c):
                u = c % 2
                sp.wait_ge(nmT_sb, both(t, c) + 1)
                for j in range(2):
                    sp.dma_start(q_st[u][64 * j + 6:64 * j + 8, :, :],
                                 nm_T[u][2 * G * j:2 * G * (j + 1), :]).then_inc(row_in[u], 16)

            def weights_load(t, u):
                e = 2 * t + u
                after(sp, w1l_done, e - 1)
                sp.dma_start(w1_raw[u][:, :], w1T[e, :, :]).then_inc(w1_in[u], 16)
                after(sp, f2_done, CH * (e - 1))
                sp.dma_start(w2_sb[u][:, :, :], w2T[e, :, :, :]).then_inc(w2_in[u], 16)

            sp.wait_ge(v_done, 1)
            load_v(0, 0)
            load_v(0, 1)
            segments(k_part, k_res, K_SEG_PART, 1, hi_done[2], mid_done[2], lo_done[2], filled_k, stack_k[1])
            rows(0, 0)
            segments(q_part, q_res, Q_SEG_PART, 1, hi_done[3], mid_done[3], lo_done[3], filled_q, stack_q[1])
            sp.wait_ge(v_done, 2)
            for u in range(2):
                weights_load(0, u)

            def step(t, c, b):
                if b + 1 < B:
                    rows(t, c + 1)
                if b + 2 < B:
                    load_v(t, c + 2)
            attention_steps(step)(sp)

            with sp.Fori(1, E // 2) as t:
                for u in range(2):
                    weights_load(t, u)

            out_v = out.rearrange("b s d -> s b d")
            for ch in range(CH):
                sp.wait_ge(acc_done, UNITS - CH + ch + 1)
                sp.dma_start(out_v[:, 4 * ch:4 * ch + 4, :], x_all[:, 4 * ch:4 * ch + 4, :]).then_inc(out_done, 16)
            sp.wait_ge(out_done, 16 * CH)

        @block.gpsimd
        def _(pool):
            steps = [0]

            def chained(ins, t=None):
                steps[0] += 1
                ins.then_inc(pool_step, 1)
                pool.wait_ge(pool_step, steps[0])

            for i, value in enumerate((EPS, -0.5)):
                nc.gpsimd.memset(consts[:, i, :], value).then_inc(filled_c, 1)
            pool.wait_ge(filled_c, 2)
            nc.gpsimd.memset(q_res[:, :, 0:HALF, :].bitcast(I32), 0).then_inc(filled_q, 1)
            nc.gpsimd.dma_start(wv_sb[:, :], Wv).then_inc(in_wv, 16)
            nc.gpsimd.dma_start(bv_sb[:, :], bv.broadcast_to([P, D])).then_inc(in_wv, 16)
            nc.gpsimd.dma_start(bo_sb[:, :], bo.broadcast_to([P, D])).then_inc(in_wo, 16)
            nc.gpsimd.dma_start(wo_sb[:, :], Wo).then_inc(in_wo, 16)

            def inv_root(w, var, count):
                n = w.shape[2]
                count(nc.gpsimd.tensor_tensor(w[:, 0, :], var, consts[:, 0, 0:n], ALU.add))
                return nc.gpsimd.tensor_tensor(w[:, 1, :], w[:, 0, :], consts[:, 1, 0:n], ALU.pow)

            def half1(w, h):
                return w[:, :, HALF * h:HALF * (h + 1)]

            for h in range(2):
                pool.wait_ge(mv1_done, HALF * (h + 1))
                inv_root(half1(rs1, h), mv1[:, HALF * h:HALF * (h + 1), 1], chained).then_inc(rstd1_done, 1)
                if h == 0:
                    nc.gpsimd.memset(v_res[:, :, :], 1.0).then_inc(filled_v, 1)
                    nc.gpsimd.memset(k_res[:, :, HALF:B, :].bitcast(I32), 0).then_inc(filled_k, 1)
                    nc.gpsimd.memset(q_res[:, :, HALF:B, :].bitcast(I32), 0).then_inc(filled_q, 1)
                    pool.wait_ge(filled_k, 2)
                    for j in range(2):
                        nc.gpsimd.dma_start(k_res[64 * j + 6:64 * j + 8, :, :, :], ones).then_inc(in_kones, 16)
                    nc.gpsimd.memset(ones_mat[:, :], 1.0).then_inc(filled_1, 1)
                    nc.gpsimd.dma_start(gam_sb[:, :], gamma).then_inc(in_misc, 16)
                    nc.gpsimd.dma_start(bet_sb[:, :], beta).then_inc(in_misc, 16)
                    nc.gpsimd.dma_start(gate_sb[:, :], gateT).then_inc(in_misc, 16)
                    nc.gpsimd.dma_start(low_sb[:, :, :], low.broadcast_to([P, E, E])).then_inc(in_misc, 16)

            base = steps[0]
            CHAIN2 = 1

            def root2(t, c):
                u = c % 2
                pool.wait_ge(mv2_done, both(t, c) + 1)
                k = [0]

                def count(ins):
                    k[0] += 1
                    ins.then_inc(pool_step, 1)
                    pool.wait_ge(pool_step, both(t, c) * CHAIN2 + (base + k[0]))
                inv_root(rs2[u], mv2[u][:, 1:2], count).then_inc(rstd2_done, 1)
                assert k[0] == CHAIN2, k[0]

            with pool.Fori(0, B // 2) as t:
                for c in range(2):
                    root2(t, c)
            steps[0] = base + B * CHAIN2
            pool.wait_ge(mv3_done, B)
            inv_root(rs3, mv3[:, :, 1], chained).then_inc(rstd3_done, 1)

        @block.scalar
        def _(act):
            def hi_part(n, bank, bias, part, h):
                act.wait_ge(proj_done[n], 1)
                nc.scalar.activation(part[:, 0, HALF * S * h:HALF * S * (h + 1)], ps[:, bank, :], ACT.Identity,
                                     bias=bias[:, 0:1]).then_inc(hi_done[n], 1)

            def mid_part(n, part, h):
                act.wait_ge(rest_done[n], 1)
                nc.scalar.activation(part[:, 1, HALF * S * h:HALF * S * (h + 1)], rest[:, n, :],
                                     ACT.Identity).then_inc(mid_done[n], 1)

            def xnT_copy(h):
                act.wait_ge(xnT_done, h + 1)
                nc.scalar.activation(xn_T[:, HALF * S * h:HALF * S * (h + 1)], ps[:, 1 + 4 * h, :],
                                     ACT.Identity).then_inc(xnT_sb, 1)

            act.wait_ge(in_wk, 32)
            hi_part(0, 0, bk_sb, k_part, 0)
            mid_part(0, k_part, 0)
            xnT_copy(0)
            act.wait_ge(in_wq, 32)
            hi_part(1, 2, bq_sb, q_part, 0)
            mid_part(1, q_part, 0)
            hi_part(2, 4, bk_sb, k_part, 1)
            mid_part(2, k_part, 1)
            xnT_copy(1)
            hi_part(3, 6, bq_sb, q_part, 1)
            mid_part(3, q_part, 1)

            def exps(t, c, h):
                b = both(t, c)
                act.wait_ge(t_done, 2 * b + h + 1)
                after(act, av_done, 2 * b + h - 1)
                nc.scalar.activation(prob[h][:, :, :, :], ps_t, ACT.Exp, scale=float(DK) ** -0.5)\
                    .then_inc(p_done, 1)

            def rows_out(t, c):
                b = both(t, c)
                act.wait_ge(nmT_done, b + 1)
                after(act, row_in[c % 2], 32 * (t + c // 2))
                nc.scalar.activation(nm_T[c % 2][:, :], ps_nm, ACT.Identity).then_inc(nmT_sb, 1)

            def oT_copy(t, c):
                b = both(t, c)
                act.wait_ge(oT_done, b + 1)
                nc.scalar.activation(o_T[c % 2][:, :], ps_oT, ACT.Identity).then_inc(oT_sb, 1)

            def x_hi(t, c):
                b = both(t, c)
                act.wait_ge(xT_done, b + 1)
                nc.scalar.activation(xf_hi[:, bass.ds(b * S, S)], ps_xT, ACT.Identity).then_inc(xhi_done, 1)

            def k_copy(t, c, b):
                if b % HALF == 0:
                    act.wait_ge(stack_k[b // HALF], 16 * SEGS)
                if b == 0:
                    act.wait_ge(in_kones, 32)
                after(act, t_done, 2 * both(t, c) - 2)
                nc.scalar.activation(k_st[c % 2][:, :, :], k_res[:, :, both(t, c), :], ACT.Identity)\
                    .then_inc(kst_done, 1)

            k_copy(0, 0, 0)
            k_copy(0, 1, 1)
            rows_out(0, 0)
            act.wait_ge(stack_k[1], 16 * SEGS)

            def step(t, c, b):
                exps(t, c, 0)
                exps(t, c, 1)
                if b + 2 < B:
                    k_copy(t, c + 2, 1)
                if b + 1 < B:
                    rows_out(t, c + 1)
                if b >= 1:
                    oT_copy(t, c - 1)
                if b >= 2:
                    x_hi(t, c - 2)
            attention_steps(step)(act)
            oT_copy(B // 2 - 1, 1)
            for c in range(2):
                x_hi(B // 2 - 1, c)

            act.wait_ge(gate_step, 7)
            nc.scalar.activation(pr[:, :, :], lg[:, 0, :, :], ACT.Exp).then_inc(lexp_done, 1)

            def gelu(t, n):
                k = 4 * t + n
                act.wait_ge(f1_done, k + 1)
                after(act, f2_done, k - 1)
                nc.scalar.activation(h_sb[n % 2][:, :, :], ps[:, 2 * (n % 2):2 * (n % 2) + 2, :], ACT.Gelu)\
                    .then_inc(gelu_done, 1)
            for n in range(4):
                gelu(0, n)
            with act.Fori(1, E // 2) as t:
                for n in range(4):
                    gelu(t, n)

        @block.vector
        def _(dve):
            nc.vector.memset(k_res[:, :, 0:HALF, :].bitcast(I32), 0).then_inc(filled_k, 1)

            def stats(h):
                dve.wait_ge(in_x[h], 16)
                for b in range(HALF * h, HALF * (h + 1)):
                    nc.vector.bn_stats(stats1[:, b, :], x_all[:, b, :]).then_inc(st1_done, 1)
                for b in range(HALF * h, HALF * (h + 1)):
                    dve.wait_ge(st1_done, b + 1)
                    nc.vector.bn_aggr(mv1[:, b, :], stats1[:, b, :]).then_inc(mv1_done, 1)

            def normal(h):
                dve.wait_ge(rstd1_done, h + 1)
                for b in range(HALF * h, HALF * (h + 1)):
                    nc.vector.tensor_scalar(xn[:, b, :], x_all[:, b, :], mv1[:, b, 0:1], rs1[:, 1, b:b + 1],
                                            ALU.subtract, ALU.mult).then_inc(xn_done, 1)

            def parts(n, bank, bias, part, h):
                dve.wait_ge(hi_done[n], 1)
                a = slice(HALF * S * h, HALF * S * (h + 1))
                nc.vector.scalar_tensor_tensor(out=rest[:, n, :], in0=ps[:, bank, :], scalar=bias[:, 0:1],
                                               in1=part[:, 0, a], op0=ALU.add, op1=ALU.subtract)\
                    .then_inc(rest_done[n], 1)
                dve.wait_ge(mid_done[n], 1)
                nc.vector.tensor_tensor(part[:, 2, a], rest[:, n, :], part[:, 1, a], ALU.subtract)\
                    .then_inc(lo_done[n], 1)

            def values(h):
                dve.wait_ge(vproj_done, h + 1)
                dve.wait_ge(filled_v, 1)
                dve.wait_ge(in_wv, 32)
                nc.vector.tensor_tensor(
                    v_res[:, HALF * h:HALF * (h + 1), 0:H * VW].rearrange("p b (h e) -> p b h e", e=VW)[:, :, :, 0:DK],
                    ps[:, 3 + 4 * h, :].rearrange("p (b h d) -> p b h d", b=HALF, d=DK),
                    bv_sb[:, :].rearrange("p (o h d) -> p o h d", o=1, d=DK).broadcast_to([P, HALF, H, DK]),
                    ALU.add).then_inc(v_done, 1)

            def q_copy(t, c):
                after(dve, t_done, 2 * both(t, c) - 2)
                nc.vector.tensor_copy(q_st[c % 2][:, :, :], q_res[:, :, both(t, c), :]).then_inc(qst_done, 1)

            stats(0)
            normal(0)
            parts(0, 0, bk_sb, k_part, 0)
            stats(1)
            parts(1, 2, bq_sb, q_part, 0)
            values(0)
            normal(1)
            parts(2, 4, bk_sb, k_part, 1)
            dve.wait_ge(in_id, 16)
            nc.vector.tensor_copy(id_bf[:, :], id_sb[:, :]).then_inc(id_ready, 1)
            dve.wait_ge(stack_q[0], 16 * SEGS)
            q_copy(0, 0)
            q_copy(0, 1)
            parts(3, 6, bq_sb, q_part, 1)
            values(1)

            dve.wait_ge(in_wo, 32)
            dve.wait_ge(xn_done, B)
            nc.vector.tensor_tensor(x_all[:, :, :], x_all[:, :, :],
                                    bo_sb[:, :].rearrange("p (o d) -> p o d", o=1).broadcast_to([P, B, D]),
                                    ALU.add).then_inc(xb_done, 1)
            dve.wait_ge(in_misc, 64)
            nc.vector.tensor_scalar(gb[:, 0, :], gate_sb[:, :], gam_sb[:, 0:1], None, ALU.mult).then_inc(gb_done, 1)
            nc.vector.tensor_scalar(gb[:, 1, :], gate_sb[:, :], bet_sb[:, 0:1], None, ALU.mult).then_inc(gb_done, 1)
            dve.wait_ge(gb_done, 2)
            nc.vector.tensor_copy(g_hi[:, :], gb[:, 0, :]).then_inc(ghi_done, 1)
            dve.wait_ge(ghi_done, 1)
            nc.vector.tensor_tensor(g_lo[:, :], gb[:, 0, :], g_hi[:, :], ALU.subtract).then_inc(glo_done, 1)
            dve.wait_ge(gsum_mm, 1)
            nc.vector.tensor_copy(gsum[:, :, :], ps_a[:, 384:384 + 2 * E].rearrange("p (a e) -> p a e", a=2))\
                .then_inc(gsum_done, 1)

            def maxima(t, c, h):
                b = both(t, c)
                dve.wait_ge(s_done, 2 * b + h + 1)
                after(dve, nm_done, b - 1)
                nc.vector.tensor_reduce(mx[c % 2][:, :, 4 * h:4 * h + 4], ps_s, AX_X, ALU.max)\
                    .then_inc(max_done, 1)

            def minus(t, c):
                b = both(t, c)
                u = c % 2
                dve.wait_ge(max_done, 2 * b + 2)
                after(dve, nmT_done, b - 1)
                nc.vector.tensor_scalar(nm[u][:, :, 0, :], mx[u][:, :, :], -1.0, None, ALU.mult).then_inc(nmh_done, 1)
                dve.wait_ge(nmh_done, b + 1)
                nc.vector.scalar_tensor_tensor(out=nm[u][:, :, 1, :], in0=mx[u][:, :, :], scalar=-1.0,
                                               in1=nm[u][:, :, 0, :], op0=ALU.mult, op1=ALU.subtract)\
                    .then_inc(nm_done, 1)

            def norm(t, c, h):
                b = both(t, c)
                dve.wait_ge(av_done, 2 * b + h + 1)
                acc = ps_o[h][:, 0:8 * VW].rearrange("p (h e) -> p h e", e=VW)
                after(dve, on_done, 2 * b + h - 1)
                nc.vector.reciprocal(rden[:, h, :], acc[:, :, DK]).then_inc(rden_done, 1)
                dve.wait_ge(rden_done, 2 * b + h + 1)
                nc.vector.tensor_tensor(
                    o_n[c % 2][:, 64 * h:64 * h + 64].rearrange("p (h d) -> p h d", d=DK), acc[:, :, 0:DK],
                    rden[:, h, :].rearrange("p (h o) -> p h o", o=1).broadcast_to([P, H // 2, DK]), ALU.mult)\
                    .then_inc(on_done, 1)

            def residual(t, c):
                b = both(t, c)
                u = c % 2
                dve.wait_ge(op_done, b + 1)
                if c < 2 and isinstance(t, int):
                    dve.wait_ge(xb_done, 1)
                nc.vector.tensor_tensor(x_all[:, b, :], ps_op, x_all[:, b, :], ALU.add).then_inc(x1_done, 1)
                dve.wait_ge(xb_done, 1)
                dve.wait_ge(x1_done, b + 1)
                nc.vector.bn_stats(stats2[u][:, :], x_all[:, b, :]).then_inc(st2_done, 1)
                dve.wait_ge(xb_done, 1)
                dve.wait_ge(st2_done, b + 1)
                nc.vector.bn_aggr(mv2[u][:, :], stats2[u][:, :]).then_inc(mv2_done, 1)

            def second_norm(t, c):
                b = both(t, c)
                u = c % 2
                dve.wait_ge(rstd2_done, b + 1)
                nc.vector.tensor_scalar(xf[u][:, :], x_all[:, b, :], mv2[u][:, 0:1], rs2[u][:, 1, :],
                                        ALU.subtract, ALU.mult).then_inc(xf_done, 1)
                dve.wait_ge(xb_done, 1)
                dve.wait_ge(xf_done, b + 1)
                nc.vector.bn_stats(stats3[:, b, :], xf[u][:, :]).then_inc(st3_done, 1)

            def x_lo(t, c):
                b = both(t, c)
                dve.wait_ge(xhi_done, b + 1)
                nc.vector.tensor_tensor(xf_lo[:, bass.ds(b * S, S)], ps_xT, xf_hi[:, bass.ds(b * S, S)],
                                        ALU.subtract).then_inc(xlo_done, 1)

            maxima(0, 0, 0)
            maxima(0, 0, 1)
            minus(0, 0)
            maxima(0, 1, 0)
            dve.wait_ge(stack_q[1], 16 * SEGS)

            def step(t, c, b):
                if b + 1 < B:
                    maxima(t, c + 1, 1)
                if b >= 1:
                    norm(t, c - 1, 1)
                if b + 1 < B:
                    minus(t, c + 1)
                norm(t, c, 0)
                if b >= 2:
                    second_norm(t, c - 2)
                if b >= 1:
                    residual(t, c - 1)
                if b >= 2:
                    x_lo(t, c - 2)
                if b + 2 < B:
                    q_copy(t, c + 2)
                    maxima(t, c + 2, 0)
            attention_steps(step)(dve)
            norm(B // 2 - 1, 1, 1)
            second_norm(B // 2 - 1, 0)
            x_lo(B // 2 - 1, 0)
            residual(B // 2 - 1, 1)
            second_norm(B // 2 - 1, 1)
            x_lo(B // 2 - 1, 1)

            def weights_split(t, u):
                e = 2 * t + u
                dve.wait_ge(w1_in[u], 16 * (t + 1))
                after(dve, f1_done, CH * (e - 1))
                nc.vector.tensor_copy(w1_hi[u][:, :], w1_raw[u][:, :]).then_inc(w1h_done, 1)
                dve.wait_ge(w1h_done, e + 1)
                nc.vector.tensor_tensor(w1_lo[u][:, :], w1_raw[u][:, :], w1_hi[u][:, :], ALU.subtract)\
                    .then_inc(w1l_done, 1)

            for u in range(2):
                weights_split(0, u)
            for b in range(B):
                dve.wait_ge(st3_done, b + 1)
                nc.vector.bn_aggr(mv3[:, b, :], stats3[:, b, :]).then_inc(mv3_done, 1)
            steps = [0]

            def chained(ins):
                steps[0] += 1
                ins.then_inc(gate_step, 1)
                dve.wait_ge(gate_step, steps[0])

            def over_e(a):
                return a.rearrange("p (b o) -> p b o", o=1).broadcast_to([P, B, E])

            def over_b(a):
                return a.rearrange("p (o e) -> p o e", o=1).broadcast_to([P, B, E])
            dve.wait_ge(mv3_done, B)
            dve.wait_ge(gsum_done, 1)
            chained(nc.vector.tensor_tensor(lg[:, 1, :, :], mv3[:, :, 0:1].broadcast_to([P, B, E]), over_b(gsum[:, 0, :]), ALU.mult))
            dve.wait_ge(lg_mm, 1)
            chained(nc.vector.tensor_tensor(lg[:, 2, :, :], ps[:, 7, 0:B * E].rearrange("p (b e) -> p b e", e=E),
                                            lg[:, 1, :, :], ALU.subtract))
            dve.wait_ge(rstd3_done, 1)
            chained(nc.vector.tensor_tensor(lg[:, 1, :, :], lg[:, 2, :, :], over_e(rs3[:, 1, :]), ALU.mult))
            chained(nc.vector.tensor_tensor(lg[:, 2, :, :], lg[:, 1, :, :], over_b(gsum[:, 1, :]), ALU.add))
            chained(nc.vector.tensor_reduce(lmax[:, :], lg[:, 2, :, :], AX_X, ALU.max))
            chained(nc.vector.tensor_tensor(lg[:, 3, :, :], lg[:, 2, :, :], over_e(lmax[:, :]), ALU.subtract))
            chained(nc.vector.tensor_copy(lg[:, 0, :, :], lg[:, 3, :, :]))
            dve.wait_ge(lexp_done, 1)
            chained(nc.vector.tensor_reduce(lsum[:, :], pr[:, :, :], AX_X, ALU.add))
            chained(nc.vector.reciprocal(lrec[:, :], lsum[:, :]))
            chained(nc.vector.tensor_tensor(lg[:, 1, :, :], pr[:, :, :], over_e(lrec[:, :]), ALU.mult))
            prob_e = lg[:, 1, :, :]
            for b in range(B):
                mine = prob_e[:, b, :].rearrange("p (e o) -> p e o", o=1).broadcast_to([P, E, E])
                their = prob_e[:, b, :].rearrange("p (o e) -> p o e", o=1).broadcast_to([P, E, E])
                nc.vector.tensor_tensor(rk[:, 0, b, :, :], their, mine, ALU.is_gt).then_inc(gate_step, 1)
                nc.vector.tensor_tensor(rk[:, 1, b, :, :], their, mine, ALU.is_equal).then_inc(gate_step, 1)
            steps[0] += 2 * B
            dve.wait_ge(gate_step, steps[0])
            low_b = low_sb[:, :, :].rearrange("p a b -> p (a b)").rearrange("p (o n) -> p o n", o=1).broadcast_to([P, B, E * E])
            eq = rk[:, 1, :, :, :].rearrange("p b a c -> p b (a c)")
            gt = rk[:, 0, :, :, :].rearrange("p b a c -> p b (a c)")
            chained(nc.vector.tensor_tensor(eq, eq, low_b, ALU.mult))
            chained(nc.vector.tensor_tensor(gt, gt, eq, ALU.add))
            chained(nc.vector.tensor_reduce(rank[:, :, :], rk[:, 0, :, :, :], AX_X, ALU.add))
            nc.vector.scalar_tensor_tensor(out=comb[:, :, :].rearrange("p b e -> p (b e)"),
                                           in0=rank[:, :, :].rearrange("p b e -> p (b e)"), scalar=1.5,
                                           in1=lg[:, 1, :, :].rearrange("p b e -> p (b e)"),
                                           op0=ALU.is_lt, op1=ALU.mult).then_inc(comb_done, 1)

            dve.wait_ge(comb_done, 1)

            def weigh(t, u):
                e = 2 * t + u
                after(dve, acc_done, CH * (e - 1))
                nc.vector.tensor_copy(cw[u][:, :], comb[:, :, e]).then_inc(cw_done, 1)
                dve.wait_ge(cw_done, e + 1)

            def accumulate(t, n):
                k = 4 * t + n
                u, ch = n // 2, n % 2
                dve.wait_ge(f2_done, k + 1)
                after(dve, acc_done, k - 1)
                for i in range(4):
                    tile = 4 * ch + i
                    last = nc.vector.scalar_tensor_tensor(
                        out=x_all[:, tile, :], in0=ps[:, 4 + n % 2, 128 * i:128 * i + 128],
                        scalar=cw[u][:, tile:tile + 1], in1=x_all[:, tile, :], op0=ALU.mult, op1=ALU.add)
                last.then_inc(acc_done, 1)

            def experts(t, more):
                for n in range(4):
                    if n % 2 == 0:
                        weigh(t, n // 2)
                    accumulate(t, n)
                    if n % 2 == 0 and more:
                        weights_split(t + 1, n // 2)
            experts(0, True)
            with dve.Fori(1, E // 2 - 1) as t:
                experts(t, True)
            experts(E // 2 - 1, False)

        @block.tensor
        def _(pe):
            def proj(n, bank, w, src, h):
                nc.tensor.matmul(ps[:, bank, :], w[:, :], src[:, HALF * S * h:HALF * S * (h + 1)],
                                 start=True, stop=True).then_inc(proj_done[n], 1)

            def turn(h):
                for b in range(HALF * h, HALF * (h + 1)):
                    pe.wait_ge(xn_done, b + 1)
                    i = b % HALF
                    last = nc.tensor.transpose(ps[:, 1 + 4 * h, 128 * i:128 * i + 128], xn[:, b, :], id_sb[:, :])
                last.then_inc(xnT_done, 1)

            def vproj(h):
                for b in range(HALF * h, HALF * (h + 1)):
                    i = b % HALF
                    last = nc.tensor.matmul(ps[:, 3 + 4 * h, 128 * i:128 * i + 128], ctx_T[:, S * b:S * b + S],
                                            wv_sb[:, :], start=True, stop=True)
                last.then_inc(vproj_done, 1)

            pe.wait_ge(in_wk, 32)
            pe.wait_ge(in_ctx, 16)
            proj(0, 0, wk_sb, ctx_T, 0)
            pe.wait_ge(in_id, 16)
            turn(0)
            proj(2, 4, wk_sb, ctx_T, 1)
            pe.wait_ge(in_wq, 32)
            pe.wait_ge(xnT_sb, 1)
            proj(1, 2, wq_sb, xn_T, 0)
            pe.wait_ge(in_wv, 32)
            vproj(0)
            turn(1)
            vproj(1)
            pe.wait_ge(xnT_sb, 2)
            proj(3, 6, wq_sb, xn_T, 1)
            pe.wait_ge(lo_done[3], 1)
            pe.wait_ge(glo_done, 1)
            pe.wait_ge(filled_1, 1)
            nc.tensor.matmul(ps_a[:, 384:384 + 2 * E], ones_mat[:, :], gb[:, :, :].rearrange("p a e -> p (a e)"),
                             start=True, stop=True).then_inc(gsum_mm, 1)

            def rows64(j):
                return slice(64 * j, 64 * j + 64)

            def scores(t, c, h):
                b = both(t, c)
                u = c % 2
                if h == 0:
                    pe.wait_ge(kst_done, b + 1)
                    pe.wait_ge(qst_done, b + 1)
                after(pe, max_done, 2 * b + h)
                for i in range(4):
                    for j in range(2):
                        last = nc.tensor.matmul(ps_s[:, j, i, :], q_st[u][rows64(j), 4 * h + i, :],
                                                k_st[u][rows64(j), 4 * h + i, :], start=True, stop=True)
                last.then_inc(s_done, 1)

            def scores_T(t, c, h):
                b = both(t, c)
                u = c % 2
                if h == 0:
                    pe.wait_ge(row_in[u], 32 * (t + c // 2 + 1))
                after(pe, p_done, 2 * b + h)
                for i in range(4):
                    for j in range(2):
                        last = nc.tensor.matmul(ps_t[:, j, i, :], k_st[u][rows64(j), 4 * h + i, :],
                                                q_st[u][rows64(j), 4 * h + i, :], start=True, stop=True)
                last.then_inc(t_done, 1)

            def minus_T(t, c, b):
                pe.wait_ge(nm_done, both(t, c) + 1)
                nc.tensor.transpose(ps_nm, nm[c % 2][:, :, :, :].rearrange("p j a g -> p (j a g)"), id_bf[:, :])\
                    .then_inc(nmT_done, 1)

            def products(t, c, h):
                b = both(t, c)
                pe.wait_ge(p_done, 2 * b + h + 1)
                if h == 0:
                    pe.wait_ge(v_in[c % 2], 16 * (t + c // 2 + 1))
                after(pe, on_done, 2 * b + h - 1)
                for i in range(8):
                    head = 8 * h + i
                    last = nc.tensor.matmul(ps_o[h][:, VW * i:VW * i + WIN], prob[h][:, head % 2, head // 2 % 4, :],
                                            v_st[c % 2][:, VW * head:VW * head + WIN], start=True, stop=True)
                last.then_inc(av_done, 1)

            def out_T(t, c):
                b = both(t, c)
                pe.wait_ge(on_done, 2 * b + 2)
                after(pe, x1_done, b)
                nc.tensor.transpose(ps_oT, o_n[c % 2][:, :], id_sb[:, :]).then_inc(oT_done, 1)

            def out_proj(t, c):
                pe.wait_ge(oT_sb, both(t, c) + 1)
                nc.tensor.matmul(ps_op, o_T[c % 2][:, :], wo_sb[:, :], start=True, stop=True).then_inc(op_done, 1)

            def turn_x(t, c, b):
                pe.wait_ge(xf_done, both(t, c) + 1)
                if b + 3 < B:
                    pe.wait_ge(nmT_sb, both(t, c) + 4)
                nc.tensor.transpose(ps_xT, xf[c % 2][:, :], id_sb[:, :]).then_inc(xT_done, 1)

            scores(0, 0, 0)
            scores(0, 0, 1)
            pe.wait_ge(id_ready, 1)
            pe.wait_ge(gsum_done, 1)
            minus_T(0, 0, 0)
            pe.wait_ge(v_done, 2)
            scores(0, 1, 0)
            pe.wait_ge(in_wo, 32)

            def step(t, c, b):
                scores_T(t, c, 0)
                if b + 1 < B:
                    scores(t, c + 1, 1)
                if b >= 1:
                    products(t, c - 1, 1)
                scores_T(t, c, 1)
                if b + 1 < B:
                    minus_T(t, c + 1, b + 1)
                if b >= 1:
                    out_T(t, c - 1)
                products(t, c, 0)
                if b >= 1:
                    out_proj(t, c - 1)
                if b >= 2:
                    turn_x(t, c - 2, b - 2)
                if b + 2 < B:
                    scores(t, c + 2, 0)
            attention_steps(step)(pe)
            products(B // 2 - 1, 1, 1)
            out_T(B // 2 - 1, 1)
            turn_x(B // 2 - 1, 0, B - 2)
            out_proj(B // 2 - 1, 1)
            turn_x(B // 2 - 1, 1, B - 1)

            pe.wait_ge(xlo_done, B)
            pe.wait_ge(x1_done, B)
            for b in range(B):
                a = slice(S * b, S * b + S)
                for i, (l, r) in enumerate(((xf_lo, g_hi), (xf_hi, g_lo), (xf_hi, g_hi))):
                    last = nc.tensor.matmul(ps[:, 7, E * b:E * b + E], l[:, a], r[:, :], start=(i == 0), stop=(i == 2))
            last.then_inc(lg_mm, 1)

            def first(t, n):
                k = 4 * t + n
                u, ch = (n // 2) % 2, n % 2
                e = 2 * t + n // 2
                pe.wait_ge(w1l_done, e + 1)
                after(pe, gelu_done, k - 1)
                a = slice(512 * ch, 512 * ch + 512)
                for fh in range(FH):
                    w = slice(P * fh, P * fh + P)
                    for i, (l, r) in enumerate(((w1_lo, xf_hi), (w1_hi, xf_lo), (w1_hi, xf_hi))):
                        last = nc.tensor.matmul(ps[:, 2 * (n % 2) + fh, :], l[u][:, w], r[:, a],
                                                start=(i == 0), stop=(i == 2))
                last.then_inc(f1_done, 1)

            def second(t, n):
                k = 4 * t + n
                u = n // 2
                pe.wait_ge(gelu_done, k + 1)
                if n % 2 == 0:
                    pe.wait_ge(w2_in[u], 16 * (t + 1))
                after(pe, acc_done, k - 1)
                for i in range(4):
                    for fh in range(FH):
                        last = nc.tensor.matmul(ps[:, 4 + n % 2, 128 * i:128 * i + 128],
                                                h_sb[n % 2][:, fh, 128 * i:128 * i + 128], w2_sb[u][:, fh, :],
                                                start=(fh == 0), stop=(fh == FH - 1))
                last.then_inc(f2_done, 1)

            first(0, 0)
            for n in range(4):
                first(0, n + 1)
                second(0, n)
            with pe.Fori(1, E // 2 - 1) as t:
                for n in range(4):
                    first(t, n + 1)
                    second(t, n)
            for n in range(4):
                if n < 3:
                    first(E // 2 - 1, n + 1)
                second(E // 2 - 1, n)


def kernel(**inputs):
    import ml_dtypes
    import numpy as np
    import concourse.bacc as bacc
    from concourse.bass_utils import run_bass_kernel_spmd as run

    a = {k: np.asarray(v) for k, v in inputs.items()}
    head_major = lambda w: w.reshape(w.shape[0], G, 2, DK).transpose(0, 2, 3, 1).reshape(w.shape[0], D)
    i32 = np.arange(E)
    arrays = {
        "x": a["x"],
        "ctxT": a["ctx_1024"].reshape(B * S, D).T,
        "Wq": head_major(a["L0_xattn_Wq"]),
        "Wk": head_major(a["L0_xattn_Wk"]),
        "Wv": a["L0_xattn_Wv"],
        "Wo": a["L0_xattn_Wo"],
        "bq": head_major(a["L0_xattn_bq"][None, :]).T,
        "bk": head_major(a["L0_xattn_bk"][None, :]).T,
        "bv": a["L0_xattn_bv"][None, :],
        "bo": a["L0_xattn_bo"][None, :],
        "gamma": a["L0_ffn_ln_gamma"][:, None],
        "beta": a["L0_ffn_ln_beta"][:, None],
        "gateT": a["L0_ffn_gate_w"].T,
        "w1T": a["L0_ffn_w1"].transpose(0, 2, 1),
        "w2T": a["L0_ffn_w2"].transpose(0, 2, 1).reshape(E, FH, P, D).transpose(0, 2, 1, 3),
        "ident": np.eye(P, dtype=np.float32),
        "low": np.tril(np.ones((E, E), np.float32), -1)[None, :, :],
        "ones": np.ones((2, B * G * S), np.float32).astype(ml_dtypes.bfloat16),
    }
    arrays = {k: np.ascontiguousarray(v) for k, v in arrays.items()}
    nc = bacc.Bacc("TRN2", target_bir_lowering=False, num_devices=1)
    args = {k: nc.dram_tensor(f"in_{k}", v.shape, mybir.dt.from_np(v.dtype), kind="ExternalInput").ap()
            for k, v in arrays.items()}
    out = nc.dram_tensor("out", (B, S, D), F32, kind="ExternalOutput").ap()
    build(nc, out=out, **args)
    r = run(nc, [{f"in_{k}": v for k, v in arrays.items()}], core_ids=[0])
    return r.results[0]["out"]
```

```python
from contextlib import ExitStack

import concourse.bass as bass
from concourse import mybir

F32 = mybir.dt.float32
F32R = mybir.dt.float32r
BF16 = mybir.dt.bfloat16
I32 = mybir.dt.int32
ALU = mybir.AluOpType
ACT = mybir.ActivationFunctionType
AX_X = mybir.AxisListType.X

P = 128
B, S, D = 8, 128, 128
H, DK = 16, 8
G = H // 2
E, F = 8, 256
FH = F // P
EPS = 1e-5
SEGS = 6
K_SEG_PART = (0, 1, 2, 0, 1, 0)
Q_SEG_PART = (0, 0, 0, 1, 1, 2)
VW = DK + 1
WIN = 128
VCOLS = H * VW + WIN - VW
HALF = 4
CH = 2
UNITS = E * CH


def build(nc, x, ctxT, pack_k, pack_v, row, w1T, w2T, ones, out):
    with ExitStack() as ctx:
        def sb(name, shape, dt=F32):
            return ctx.enter_context(nc.sbuf_tensor(name, shape, dt))

        def sem(name):
            return ctx.enter_context(nc.semaphore(name))

        x_all = sb("x_all", [P, B, D])
        ctx_T = sb("ctx_T", [P, B * S])
        pk = sb("pk", [P, 3 * D + 4 + E])
        wk_sb, wq_sb, id_sb = (pk[:, D * i:D * i + D] for i in range(3))
        bk_sb, bq_sb, gam_sb, bet_sb = (pk[:, 3 * D + i:3 * D + i + 1] for i in range(4))
        gate_sb = pk[:, 3 * D + 4:3 * D + 4 + E]
        pv = sb("pv", [P, 2 * D])
        wv_sb, wo_sb = pv[:, 0:D], pv[:, D:2 * D]
        rw = sb("rw", [P, 2 * D + E * E])
        bv_sb, bo_sb = rw[:, 0:D], rw[:, D:2 * D]
        low_sb = rw[:, 2 * D:2 * D + E * E]
        id_bf = sb("id_bf", [P, P], BF16)
        ones_mat = sb("ones_mat", [P, P])
        stats1 = sb("stats1", [P, B, 6])
        mv1 = sb("mv1", [P, B, 2])
        consts = sb("consts", [P, 3, B])
        warm = sb("warm", [P, 1])
        rs1 = sb("rs1", [P, 2, B])
        xn = sb("xn", [P, B, D])
        xn_T = sb("xn_T", [P, B * S])
        k_part = sb("k_part", [P, 3, B * S], BF16)
        q_part = sb("q_part", [P, 3, B * S], BF16)
        rest = sb("rest", [P, 4, HALF * S])
        k_res = sb("k_res", [P, G, B, S], BF16)
        q_res = sb("q_res", [P, G, B, S], BF16)
        v_res = sb("v_res", [P, B, VCOLS])
        k_st = [sb(f"k_st{u}", [P, G, S], BF16) for u in range(2)]
        q_st = [sb(f"q_st{u}", [P, G, S], BF16) for u in range(2)]
        v_st = [sb(f"v_st{u}", [P, VCOLS]) for u in range(2)]
        mx = [sb(f"mx{u}", [P, 2, G]) for u in range(2)]
        nm = [sb(f"nm{u}", [P, 2, 2, G], BF16) for u in range(2)]
        nm_T = [sb(f"nm_T{u}", [4 * G, S], BF16) for u in range(2)]
        prob = [sb(f"prob{h}", [P, 2, G // 2, S]) for h in range(2)]
        rden = sb("rden", [P, 2, H // 2])
        o_n = [sb(f"o_n{u}", [P, D]) for u in range(2)]
        o_T = [sb(f"o_T{u}", [P, S]) for u in range(2)]
        stats2 = [sb(f"stats2{u}", [P, 6]) for u in range(2)]
        mv2 = [sb(f"mv2{u}", [P, 2]) for u in range(2)]
        rs2 = [sb(f"rs2{u}", [P, 4, 1]) for u in range(2)]
        xf = [sb(f"xf{u}", [P, D]) for u in range(2)]
        xf_T = sb("xf_T", [P, B * S])
        stats3 = sb("stats3", [P, B, 6])
        mv3 = sb("mv3", [P, B, 2])
        rs3 = sb("rs3", [P, 2, B])
        xf_hi = sb("xf_hi", [P, B * S], F32R)
        xf_lo = sb("xf_lo", [P, B * S], F32R)
        gb = sb("gb", [P, 2, E])
        lg = sb("lg", [P, 4, B, E])
        lmax, lsum, lrec = sb("lmax", [P, B]), sb("lsum", [P, B]), sb("lrec", [P, B])
        pr = sb("pr", [P, B, E])
        rk = sb("rk", [P, 2, B, E, E])
        rank = sb("rank", [P, B, E])
        comb = sb("comb", [P, B, E])
        w1_raw = [sb(f"w1_raw{u}", [P, F]) for u in range(2)]
        w1_hi = [sb(f"w1_hi{u}", [P, F], F32R) for u in range(2)]
        w1_lo = [sb(f"w1_lo{u}", [P, F], F32R) for u in range(2)]
        w2_sb = [sb(f"w2_sb{u}", [P, FH, D]) for u in range(2)]
        h_sb = [sb(f"h_sb{u}", [P, FH, 512]) for u in range(2)]
        cw = [sb(f"cw{u}", [P, B]) for u in range(2)]

        ps = ctx.enter_context(nc.psum_tensor("ps", [P, 8, 512], F32))
        ps_s = ps[:, 0:2, :].rearrange("p j (g n) -> p j g n", n=S)
        ps_t = ps[:, 2:4, :].rearrange("p j (g n) -> p j g n", n=S)
        ps_o = [ps[:, 4 + h, :] for h in range(2)]
        ps_a, ps_b = ps[:, 6, :], ps[:, 7, :]
        ps_nm = ps_a[0:4 * G, 0:S // 2].bitcast(BF16)
        ps_xT = ps_a[:, 128:256]
        ps_oT, ps_op = ps_b[:, 0:128], ps_b[:, 128:256]
        ps_lg = ps_b[:, 256:256 + B * E]
        ps_gs = ps_b[:, 384:384 + 2 * E]

        in_x = [sem(f"in_x{h}") for h in range(2)]
        in_ctx = [sem(f"in_ctx{h}") for h in range(2)]
        in_pk, in_pv, in_rw = sem("in_pk"), sem("in_pv"), sem("in_rw")
        in_kones = sem("in_kones")
        filled_c, filled_k, filled_q, filled_v, filled_1 = sem("filled_c"), sem("filled_k"), sem("filled_q"), sem("filled_v"), sem("filled_1")
        id_ready, warm_done = sem("id_ready"), sem("warm_done")
        st1_done, mv1_done, rstd1_done, xn_done = sem("st1_done"), sem("mv1_done"), sem("rstd1_done"), sem("xn_done")
        pool_step = sem("pool_step")
        xnT_done, xnT_sb = sem("xnT_done"), sem("xnT_sb")
        proj_done = [sem(f"proj{n}_done") for n in range(4)]
        hi_done = [sem(f"hi{n}_done") for n in range(4)]
        rest_done = [sem(f"rest{n}_done") for n in range(4)]
        mid_done = [sem(f"mid{n}_done") for n in range(4)]
        lo_done = [sem(f"lo{n}_done") for n in range(4)]
        stack_k = [sem(f"stack_k{h}") for h in range(2)]
        stack_q = [sem(f"stack_q{h}") for h in range(2)]
        vproj_done, v_done = sem("vproj_done"), sem("v_done")
        v_in = [sem(f"v_in{u}") for u in range(2)]
        kst_done, qst_done = sem("kst_done"), sem("qst_done")
        row_in = [sem(f"row_in{u}") for u in range(2)]
        s_done, max_done, nmh_done, nm_done, nmT_done, nmT_sb = (
            sem(n) for n in ("s_done", "max_done", "nmh_done", "nm_done", "nmT_done", "nmT_sb"))
        t_done, p_done, av_done, rden_done, on_done = (
            sem(n) for n in ("t_done", "p_done", "av_done", "rden_done", "on_done"))
        oT_done, oT_sb, op_done, x1_done, st2_done, mv2_done, rstd2_done, xf_done, st3_done = (
            sem(n) for n in ("oT_done", "oT_sb", "op_done", "x1_done", "st2_done", "mv2_done", "rstd2_done",
                             "xf_done", "st3_done"))
        xT_done, xT_sb, xhi_done, xlo_done, xb_done = sem("xT_done"), sem("xT_sb"), sem("xhi_done"), sem("xlo_done"), sem("xb_done")
        gb_done = sem("gb_done")
        mv3_done, rstd3_done, lg_mm, gate_step, lexp_done, comb_done = (
            sem(n) for n in ("mv3_done", "rstd3_done", "lg_mm", "gate_step", "lexp_done", "comb_done"))
        w1_in = [sem(f"w1_in{u}") for u in range(2)]
        w2_in = [sem(f"w2_in{u}") for u in range(2)]
        w1h_done, w1l_done = sem("w1h_done"), sem("w1l_done")
        f1_done, gelu_done, f2_done, cw_done, acc_done = (
            sem(n) for n in ("f1_done", "gelu_done", "f2_done", "cw_done", "acc_done"))
        out_done = sem("out_done")

        block = ctx.enter_context(nc.Block())

        def after(eng, s, n):
            if not isinstance(n, int) or n > 0:
                eng.wait_ge(s, n)

        def both(t, c):
            return 2 * t + c

        def attention_steps(step):
            def run(eng):
                for c in range(2):
                    step(0, c, c)
                with eng.Fori(1, B // 2 - 1) as t:
                    for c in range(2):
                        step(t, c, 2 + c)
                for c in range(2):
                    step(B // 2 - 1, c, B - 2 + c)
            return run


        @block.sync
        def _(sp):
            x_v = x.rearrange("b s d -> s b d")
            for h in range(2):
                a = slice(HALF * S * h, HALF * S * (h + 1))
                sp.dma_start(x_all[:, HALF * h:HALF * (h + 1), :], x_v[:, HALF * h:HALF * (h + 1), :])\
                    .then_inc(in_x[h], 16)
                if h == 0:
                    sp.dma_start(pk[:, :], pack_k).then_inc(in_pk, 16)
                sp.dma_start(ctx_T[:, a], ctxT[:, a]).then_inc(in_ctx[h], 16)
                if h == 0:
                    sp.dma_start(pv[:, :], pack_v).then_inc(in_pv, 16)
                    sp.dma_start(rw[:, :], row.broadcast_to([P, 2 * D + E * E])).then_inc(in_rw, 16)

            def segments(part, res, seg_part, h, hi, rst, lo, fill, done):
                for want, (s_ready) in ((0, hi), (1, rst), (2, lo)):
                    for s in range(SEGS):
                        if seg_part[s] == want:
                            sp.wait_ge(s_ready, 1)
                            sp.wait_ge(fill, 1 + h)
                            dst = res[s:P:DK, :, HALF * h:HALF * (h + 1), :].rearrange("p g b n -> p g (b n)")
                            src = part[:, want, HALF * S * h:HALF * S * (h + 1)]
                            sp.dma_start(dst, src).then_inc(done, 16)

            segments(k_part, k_res, K_SEG_PART, 0, hi_done[0], mid_done[0], lo_done[0], filled_k, stack_k[0])
            segments(q_part, q_res, Q_SEG_PART, 0, hi_done[1], mid_done[1], lo_done[1], filled_q, stack_q[0])

            def load_v(t, c):
                u = c % 2
                after(sp, av_done, 2 * both(t, c) - 2)
                sp.dma_start(v_st[u][:, :], v_res[:, both(t, c), :]).then_inc(v_in[u], 16)

            def rows(t, c):
                u = c % 2
                sp.wait_ge(nmT_sb, both(t, c) + 1)
                for j in range(2):
                    sp.dma_start(q_st[u][64 * j + 6:64 * j + 8, :, :],
                                 nm_T[u][2 * G * j:2 * G * (j + 1), :]).then_inc(row_in[u], 16)

            def weights_load(t, u):
                e = 2 * t + u
                after(sp, w1l_done, e - 1)
                sp.dma_start(w1_raw[u][:, :], w1T[e, :, :]).then_inc(w1_in[u], 16)
                after(sp, f2_done, CH * (e - 1))
                sp.dma_start(w2_sb[u][:, :, :], w2T[e, :, :, :]).then_inc(w2_in[u], 16)

            sp.wait_ge(v_done, 1)
            load_v(0, 0)
            load_v(0, 1)
            segments(k_part, k_res, K_SEG_PART, 1, hi_done[2], mid_done[2], lo_done[2], filled_k, stack_k[1])
            rows(0, 0)
            segments(q_part, q_res, Q_SEG_PART, 1, hi_done[3], mid_done[3], lo_done[3], filled_q, stack_q[1])
            sp.wait_ge(v_done, 2)
            for u in range(2):
                weights_load(0, u)

            def step(t, c, b):
                if b + 1 < B:
                    rows(t, c + 1)
                if b + 2 < B:
                    load_v(t, c + 2)
            attention_steps(step)(sp)

            with sp.Fori(1, E // 2) as t:
                for u in range(2):
                    weights_load(t, u)

            out_v = out.rearrange("b s d -> s b d")
            for ch in range(CH):
                sp.wait_ge(acc_done, UNITS - CH + ch + 1)
                sp.dma_start(out_v[:, 4 * ch:4 * ch + 4, :], x_all[:, 4 * ch:4 * ch + 4, :]).then_inc(out_done, 16)
            sp.wait_ge(out_done, 16 * CH)

        @block.gpsimd
        def _(pool):
            steps = [0]

            def chained(ins, t=None):
                steps[0] += 1
                ins.then_inc(pool_step, 1)
                pool.wait_ge(pool_step, steps[0])

            for i, value in enumerate((EPS, -0.5, -1.0)):
                nc.gpsimd.memset(consts[:, i, :], value).then_inc(filled_c, 1)
            pool.wait_ge(filled_c, 3)
            nc.gpsimd.memset(q_res[:, :, 0:HALF, :].bitcast(I32), 0).then_inc(filled_q, 1)
            def inv_root(w, var, count):
                n = w.shape[2]
                count(nc.gpsimd.tensor_tensor(w[:, 0, :], var, consts[:, 0, 0:n], ALU.add))
                return nc.gpsimd.tensor_tensor(w[:, 1, :], w[:, 0, :], consts[:, 1, 0:n], ALU.pow)

            def half1(w, h):
                return w[:, :, HALF * h:HALF * (h + 1)]

            def root1(h):
                pool.wait_ge(mv1_done, HALF * (h + 1))
                inv_root(half1(rs1, h), mv1[:, HALF * h:HALF * (h + 1), 1], chained).then_inc(rstd1_done, 1)

            root1(0)
            nc.gpsimd.memset(v_res[:, 0:HALF, :], 1.0).then_inc(filled_v, 1)
            nc.gpsimd.memset(k_res[:, :, HALF:B, :].bitcast(I32), 0).then_inc(filled_k, 1)
            pool.wait_ge(filled_k, 2)
            for j in range(2):
                nc.gpsimd.dma_start(k_res[64 * j + 6:64 * j + 8, :, :, :], ones).then_inc(in_kones, 16)
            root1(1)
            nc.gpsimd.memset(q_res[:, :, HALF:B, :].bitcast(I32), 0).then_inc(filled_q, 1)
            nc.gpsimd.memset(v_res[:, HALF:B, :], 1.0).then_inc(filled_v, 1)
            nc.gpsimd.memset(ones_mat[:, :], 1.0).then_inc(filled_1, 1)
            pool.wait_ge(xn_done, B)
            pool.wait_ge(in_rw, 16)
            nc.gpsimd.tensor_tensor(x_all[:, :, :], x_all[:, :, :],
                                    bo_sb.rearrange("p (o d) -> p o d", o=1).broadcast_to([P, B, D]),
                                    ALU.add).then_inc(xb_done, 1)

            base = steps[0]
            CHAIN2 = 3

            def root2(t, c):
                u = c % 2
                b = both(t, c)
                pool.wait_ge(mv2_done, b + 1)
                k = [0]

                def count(ins):
                    k[0] += 1
                    ins.then_inc(pool_step, 1)
                    pool.wait_ge(pool_step, b * CHAIN2 + (base + k[0]))
                after(pool, xf_done, b - 1)
                count(inv_root(rs2[u], mv2[u][:, 1:2], count))
                count(nc.gpsimd.tensor_tensor(rs2[u][:, 2, :], mv2[u][:, 0:1], consts[:, 2, 0:1], ALU.mult))
                nc.gpsimd.tensor_tensor(rs2[u][:, 3, :], rs2[u][:, 2, :], rs2[u][:, 1, :], ALU.mult)\
                    .then_inc(rstd2_done, 1)
                assert k[0] == CHAIN2, k[0]

            def x_lo(t, c):
                b = both(t, c)
                pool.wait_ge(xT_sb, b + 1)
                nc.gpsimd.tensor_tensor(xf_lo[:, bass.ds(b * S, S)], xf_T[:, bass.ds(b * S, S)], xf_hi[:, bass.ds(b * S, S)],
                                        ALU.subtract).then_inc(xlo_done, 1)

            for c in range(2):
                root2(0, c)
            with pool.Fori(1, B // 2) as t:
                for c in range(2):
                    x_lo(t, c - 2)
                    root2(t, c)
            for c in range(2):
                x_lo(B // 2 - 1, c)
            steps[0] = base + B * CHAIN2
            pool.wait_ge(mv3_done, B)
            inv_root(rs3, mv3[:, :, 1], chained).then_inc(rstd3_done, 1)

        @block.scalar
        def _(act):
            def hi_part(n, bank, bias, part, h):
                act.wait_ge(proj_done[n], 1)
                nc.scalar.activation(part[:, 0, HALF * S * h:HALF * S * (h + 1)], ps[:, bank, :], ACT.Identity,
                                     bias=bias).then_inc(hi_done[n], 1)

            def mid_part(n, part, h):
                act.wait_ge(rest_done[n], 1)
                nc.scalar.activation(part[:, 1, HALF * S * h:HALF * S * (h + 1)], rest[:, n, :],
                                     ACT.Identity).then_inc(mid_done[n], 1)

            def xnT_copy(h):
                act.wait_ge(xnT_done, h + 1)
                nc.scalar.activation(xn_T[:, HALF * S * h:HALF * S * (h + 1)], ps[:, 1 + 4 * h, :],
                                     ACT.Identity).then_inc(xnT_sb, 1)

            act.wait_ge(filled_c, 1)
            nc.scalar.activation(warm[:, :], consts[:, 0, 0:1], ACT.Exp).then_inc(warm_done, 1)
            act.wait_ge(in_pk, 16)
            hi_part(0, 0, bk_sb, k_part, 0)
            mid_part(0, k_part, 0)
            xnT_copy(0)
            hi_part(1, 2, bq_sb, q_part, 0)
            hi_part(2, 4, bk_sb, k_part, 1)
            mid_part(1, q_part, 0)
            mid_part(2, k_part, 1)
            xnT_copy(1)

            def exps(t, c, h):
                b = both(t, c)
                act.wait_ge(t_done, 2 * b + h + 1)
                after(act, av_done, 2 * b + h - 1)
                nc.scalar.activation(prob[h][:, :, :, :], ps_t, ACT.Exp, scale=float(DK) ** -0.5)\
                    .then_inc(p_done, 1)

            def second_norm(t, c):
                b = both(t, c)
                act.wait_ge(rstd2_done, b + 1)
                nc.scalar.activation(xf[c % 2][:, :], x_all[:, b, :], ACT.Identity, scale=rs2[c % 2][:, 1, :],
                                     bias=rs2[c % 2][:, 3, :]).then_inc(xf_done, 1)

            def rows_out(t, c):
                b = both(t, c)
                act.wait_ge(nmT_done, b + 1)
                after(act, row_in[c % 2], 32 * (t + c // 2))
                nc.scalar.activation(nm_T[c % 2][:, :], ps_nm, ACT.Identity).then_inc(nmT_sb, 1)

            def oT_copy(t, c):
                b = both(t, c)
                act.wait_ge(oT_done, b + 1)
                nc.scalar.activation(o_T[c % 2][:, :], ps_oT, ACT.Identity).then_inc(oT_sb, 1)

            def x_T(t, c):
                b = both(t, c)
                act.wait_ge(xT_done, b + 1)
                nc.scalar.activation(xf_hi[:, bass.ds(b * S, S)], ps_xT, ACT.Identity).then_inc(xhi_done, 1)
                nc.scalar.activation(xf_T[:, bass.ds(b * S, S)], ps_xT, ACT.Identity).then_inc(xT_sb, 1)

            def k_copy(t, c, b):
                if b % HALF == 0:
                    act.wait_ge(stack_k[b // HALF], 16 * SEGS)
                if b == 0:
                    act.wait_ge(in_kones, 32)
                after(act, t_done, 2 * both(t, c) - 2)
                nc.scalar.activation(k_st[c % 2][:, :, :], k_res[:, :, both(t, c), :], ACT.Identity)\
                    .then_inc(kst_done, 1)

            k_copy(0, 0, 0)
            k_copy(0, 1, 1)
            rows_out(0, 0)
            hi_part(3, 5, bq_sb, q_part, 1)
            mid_part(3, q_part, 1)
            act.wait_ge(stack_k[1], 16 * SEGS)

            def step(t, c, b):
                exps(t, c, 0)
                if b >= 2:
                    second_norm(t, c - 2)
                if b + 1 < B:
                    rows_out(t, c + 1)
                if b >= 1:
                    oT_copy(t, c - 1)
                exps(t, c, 1)
                if b + 2 < B:
                    k_copy(t, c + 2, 1)
                if b >= 2:
                    x_T(t, c - 2)
            attention_steps(step)(act)
            last = B // 2 - 1
            second_norm(last, 0)
            oT_copy(last, 1)
            x_T(last, 0)
            second_norm(last, 1)
            x_T(last, 1)

            act.wait_ge(gate_step, 7)
            nc.scalar.activation(pr[:, :, :], lg[:, 0, :, :], ACT.Exp).then_inc(lexp_done, 1)

            def gelu(t, n):
                k = 4 * t + n
                act.wait_ge(f1_done, k + 1)
                after(act, f2_done, k - 1)
                nc.scalar.activation(h_sb[n % 2][:, :, :], ps[:, 2 * (n % 2):2 * (n % 2) + 2, :], ACT.Gelu)\
                    .then_inc(gelu_done, 1)
            for n in range(4):
                gelu(0, n)
            with act.Fori(1, E // 2) as t:
                for n in range(4):
                    gelu(t, n)

        @block.vector
        def _(dve):
            nc.vector.memset(k_res[:, :, 0:HALF, :].bitcast(I32), 0).then_inc(filled_k, 1)

            def stats(h):
                dve.wait_ge(in_x[h], 16)
                for b in range(HALF * h, HALF * (h + 1)):
                    nc.vector.bn_stats(stats1[:, b, :], x_all[:, b, :]).then_inc(st1_done, 1)
                for b in range(HALF * h, HALF * (h + 1)):
                    dve.wait_ge(st1_done, b + 1)
                    nc.vector.bn_aggr(mv1[:, b, :], stats1[:, b, :]).then_inc(mv1_done, 1)

            def normal(h):
                dve.wait_ge(rstd1_done, h + 1)
                for b in range(HALF * h, HALF * (h + 1)):
                    nc.vector.tensor_scalar(xn[:, b, :], x_all[:, b, :], mv1[:, b, 0:1], rs1[:, 1, b:b + 1],
                                            ALU.subtract, ALU.mult).then_inc(xn_done, 1)

            def parts(n, bank, bias, part, h):
                dve.wait_ge(hi_done[n], 1)
                a = slice(HALF * S * h, HALF * S * (h + 1))
                nc.vector.scalar_tensor_tensor(out=rest[:, n, :], in0=ps[:, bank, :], scalar=bias,
                                               in1=part[:, 0, a], op0=ALU.add, op1=ALU.subtract)\
                    .then_inc(rest_done[n], 1)
                dve.wait_ge(mid_done[n], 1)
                nc.vector.tensor_tensor(part[:, 2, a], rest[:, n, :], part[:, 1, a], ALU.subtract)\
                    .then_inc(lo_done[n], 1)

            def values(h):
                dve.wait_ge(vproj_done, h + 1)
                dve.wait_ge(filled_v, h + 1)
                dve.wait_ge(in_rw, 16)
                nc.vector.tensor_tensor(
                    v_res[:, HALF * h:HALF * (h + 1), 0:H * VW].rearrange("p b (h e) -> p b h e", e=VW)[:, :, :, 0:DK],
                    ps[:, 3 + 4 * h, :].rearrange("p (b h d) -> p b h d", b=HALF, d=DK),
                    bv_sb.rearrange("p (o h d) -> p o h d", o=1, d=DK).broadcast_to([P, HALF, H, DK]),
                    ALU.add).then_inc(v_done, 1)

            def q_copy(t, c):
                after(dve, t_done, 2 * both(t, c) - 2)
                nc.vector.tensor_copy(q_st[c % 2][:, :, :], q_res[:, :, both(t, c), :]).then_inc(qst_done, 1)

            stats(0)
            normal(0)
            parts(0, 0, bk_sb, k_part, 0)
            stats(1)
            parts(1, 2, bq_sb, q_part, 0)
            values(0)
            normal(1)
            parts(2, 4, bk_sb, k_part, 1)
            dve.wait_ge(in_pk, 16)
            nc.vector.tensor_copy(id_bf[:, :], id_sb).then_inc(id_ready, 1)
            dve.wait_ge(stack_q[0], 16 * SEGS)
            q_copy(0, 0)
            q_copy(0, 1)
            nc.vector.tensor_scalar(gb[:, 0, :], gate_sb, gam_sb, None, ALU.mult).then_inc(gb_done, 1)
            nc.vector.tensor_scalar(gb[:, 1, :], gate_sb, bet_sb, None, ALU.mult).then_inc(gb_done, 1)

            def maxima(t, c, h):
                b = both(t, c)
                dve.wait_ge(s_done, 2 * b + h + 1)
                after(dve, nm_done, b - 1)
                nc.vector.tensor_reduce(mx[c % 2][:, :, 4 * h:4 * h + 4], ps_s, AX_X, ALU.max)\
                    .then_inc(max_done, 1)

            def minus(t, c):
                b = both(t, c)
                u = c % 2
                dve.wait_ge(max_done, 2 * b + 2)
                after(dve, nmT_done, b - 1)
                nc.vector.tensor_scalar(nm[u][:, :, 0, :], mx[u][:, :, :], -1.0, None, ALU.mult).then_inc(nmh_done, 1)
                dve.wait_ge(nmh_done, b + 1)
                nc.vector.scalar_tensor_tensor(out=nm[u][:, :, 1, :], in0=mx[u][:, :, :], scalar=-1.0,
                                               in1=nm[u][:, :, 0, :], op0=ALU.mult, op1=ALU.subtract)\
                    .then_inc(nm_done, 1)

            def norm(t, c):
                b = both(t, c)
                dve.wait_ge(av_done, 2 * b + 2)
                acc = ps[:, 4:6, 0:8 * VW].rearrange("p a (h e) -> p a h e", e=VW)
                after(dve, on_done, b)
                nc.vector.reciprocal(rden[:, :, :], acc[:, :, :, DK]).then_inc(rden_done, 1)
                dve.wait_ge(rden_done, b + 1)
                nc.vector.tensor_tensor(
                    o_n[c % 2][:, :].rearrange("p (a h d) -> p a h d", a=2, d=DK), acc[:, :, :, 0:DK],
                    rden[:, :, :].rearrange("p a (h o) -> p a h o", o=1).broadcast_to([P, 2, H // 2, DK]), ALU.mult)\
                    .then_inc(on_done, 1)

            def residual(t, c):
                b = both(t, c)
                u = c % 2
                dve.wait_ge(op_done, b + 1)
                if c < 2 and isinstance(t, int):
                    dve.wait_ge(xb_done, 1)
                nc.vector.tensor_tensor(x_all[:, b, :], ps_op, x_all[:, b, :], ALU.add).then_inc(x1_done, 1)
                dve.wait_ge(xb_done, 1)
                dve.wait_ge(x1_done, b + 1)
                nc.vector.bn_stats(stats2[u][:, :], x_all[:, b, :]).then_inc(st2_done, 1)
                dve.wait_ge(xb_done, 1)
                dve.wait_ge(st2_done, b + 1)
                nc.vector.bn_aggr(mv2[u][:, :], stats2[u][:, :]).then_inc(mv2_done, 1)

            def stats_xf(t, c):
                b = both(t, c)
                dve.wait_ge(xb_done, 1)
                dve.wait_ge(xf_done, b + 1)
                nc.vector.bn_stats(stats3[:, b, :], xf[c % 2][:, :]).then_inc(st3_done, 1)

            maxima(0, 0, 0)
            maxima(0, 0, 1)
            minus(0, 0)
            parts(3, 5, bq_sb, q_part, 1)
            maxima(0, 1, 0)
            values(1)
            dve.wait_ge(stack_q[1], 16 * SEGS)

            def step(t, c, b):
                if b + 1 < B:
                    maxima(t, c + 1, 1)
                    minus(t, c + 1)
                if b >= 1:
                    norm(t, c - 1)
                if b + 2 < B:
                    q_copy(t, c + 2)
                if b >= 2:
                    stats_xf(t, c - 2)
                if b >= 1:
                    residual(t, c - 1)
                if b + 2 < B:
                    maxima(t, c + 2, 0)
            attention_steps(step)(dve)
            last = B // 2 - 1
            norm(last, 1)
            stats_xf(last, 0)
            residual(last, 1)
            stats_xf(last, 1)

            def weights_split(t, u):
                e = 2 * t + u
                dve.wait_ge(w1_in[u], 16 * (t + 1))
                after(dve, f1_done, CH * (e - 1))
                nc.vector.tensor_copy(w1_hi[u][:, :], w1_raw[u][:, :]).then_inc(w1h_done, 1)
                dve.wait_ge(w1h_done, e + 1)
                nc.vector.tensor_tensor(w1_lo[u][:, :], w1_raw[u][:, :], w1_hi[u][:, :], ALU.subtract)\
                    .then_inc(w1l_done, 1)

            for u in range(2):
                weights_split(0, u)
            for b in range(B):
                dve.wait_ge(st3_done, b + 1)
                nc.vector.bn_aggr(mv3[:, b, :], stats3[:, b, :]).then_inc(mv3_done, 1)
            steps = [0]

            def chained(ins):
                steps[0] += 1
                ins.then_inc(gate_step, 1)
                dve.wait_ge(gate_step, steps[0])

            def over_e(a):
                return a.rearrange("p (b o) -> p b o", o=1).broadcast_to([P, B, E])

            def over_b(a):
                return a.rearrange("p (o e) -> p o e", o=1).broadcast_to([P, B, E])
            dve.wait_ge(mv3_done, B)
            dve.wait_ge(lg_mm, 1)
            chained(nc.vector.tensor_tensor(lg[:, 1, :, :], mv3[:, :, 0:1].broadcast_to([P, B, E]), over_b(ps_gs[:, 0:E]), ALU.mult))
            chained(nc.vector.tensor_tensor(lg[:, 2, :, :], ps_lg.rearrange("p (b e) -> p b e", e=E),
                                            lg[:, 1, :, :], ALU.subtract))
            dve.wait_ge(rstd3_done, 1)
            chained(nc.vector.tensor_tensor(lg[:, 1, :, :], lg[:, 2, :, :], over_e(rs3[:, 1, :]), ALU.mult))
            chained(nc.vector.tensor_tensor(lg[:, 2, :, :], lg[:, 1, :, :], over_b(ps_gs[:, E:2 * E]), ALU.add))
            chained(nc.vector.tensor_reduce(lmax[:, :], lg[:, 2, :, :], AX_X, ALU.max))
            chained(nc.vector.tensor_tensor(lg[:, 3, :, :], lg[:, 2, :, :], over_e(lmax[:, :]), ALU.subtract))
            chained(nc.vector.tensor_copy(lg[:, 0, :, :], lg[:, 3, :, :]))
            dve.wait_ge(lexp_done, 1)
            chained(nc.vector.tensor_reduce(lsum[:, :], pr[:, :, :], AX_X, ALU.add))
            chained(nc.vector.reciprocal(lrec[:, :], lsum[:, :]))
            chained(nc.vector.tensor_tensor(lg[:, 1, :, :], pr[:, :, :], over_e(lrec[:, :]), ALU.mult))
            prob_e = lg[:, 1, :, :]
            for b in range(B):
                mine = prob_e[:, b, :].rearrange("p (e o) -> p e o", o=1).broadcast_to([P, E, E])
                their = prob_e[:, b, :].rearrange("p (o e) -> p o e", o=1).broadcast_to([P, E, E])
                nc.vector.tensor_tensor(rk[:, 0, b, :, :], their, mine, ALU.is_gt).then_inc(gate_step, 1)
                nc.vector.tensor_tensor(rk[:, 1, b, :, :], their, mine, ALU.is_equal).then_inc(gate_step, 1)
            steps[0] += 2 * B
            dve.wait_ge(gate_step, steps[0])
            low_b = low_sb.rearrange("p (o n) -> p o n", o=1).broadcast_to([P, B, E * E])
            eq = rk[:, 1, :, :, :].rearrange("p b a c -> p b (a c)")
            gt = rk[:, 0, :, :, :].rearrange("p b a c -> p b (a c)")
            chained(nc.vector.tensor_tensor(eq, eq, low_b, ALU.mult))
            chained(nc.vector.tensor_tensor(gt, gt, eq, ALU.add))
            chained(nc.vector.tensor_reduce(rank[:, :, :], rk[:, 0, :, :, :], AX_X, ALU.add))
            nc.vector.scalar_tensor_tensor(out=comb[:, :, :].rearrange("p b e -> p (b e)"),
                                           in0=rank[:, :, :].rearrange("p b e -> p (b e)"), scalar=1.5,
                                           in1=lg[:, 1, :, :].rearrange("p b e -> p (b e)"),
                                           op0=ALU.is_lt, op1=ALU.mult).then_inc(comb_done, 1)

            dve.wait_ge(comb_done, 1)

            def weigh(t, u):
                e = 2 * t + u
                after(dve, acc_done, CH * (e - 1))
                nc.vector.tensor_copy(cw[u][:, :], comb[:, :, e]).then_inc(cw_done, 1)
                dve.wait_ge(cw_done, e + 1)

            def accumulate(t, n):
                k = 4 * t + n
                u, ch = n // 2, n % 2
                dve.wait_ge(f2_done, k + 1)
                after(dve, acc_done, k - 1)
                for i in range(4):
                    tile = 4 * ch + i
                    last = nc.vector.scalar_tensor_tensor(
                        out=x_all[:, tile, :], in0=ps[:, 4 + n % 2, 128 * i:128 * i + 128],
                        scalar=cw[u][:, tile:tile + 1], in1=x_all[:, tile, :], op0=ALU.mult, op1=ALU.add)
                last.then_inc(acc_done, 1)

            def experts(t, more):
                for n in range(4):
                    if n % 2 == 0:
                        weigh(t, n // 2)
                    accumulate(t, n)
                    if n % 2 == 0 and more:
                        weights_split(t + 1, n // 2)
            experts(0, True)
            with dve.Fori(1, E // 2 - 1) as t:
                experts(t, True)
            experts(E // 2 - 1, False)

        @block.tensor
        def _(pe):
            def proj(n, bank, w, src, h):
                nc.tensor.matmul(ps[:, bank, :], w, src[:, HALF * S * h:HALF * S * (h + 1)],
                                 start=True, stop=True).then_inc(proj_done[n], 1)

            def turn(h):
                for b in range(HALF * h, HALF * (h + 1)):
                    pe.wait_ge(xn_done, b + 1)
                    i = b % HALF
                    last = nc.tensor.transpose(ps[:, 1 + 4 * h, 128 * i:128 * i + 128], xn[:, b, :], id_sb)
                last.then_inc(xnT_done, 1)

            def vproj(h):
                for b in range(HALF * h, HALF * (h + 1)):
                    i = b % HALF
                    last = nc.tensor.matmul(ps[:, 3 + 4 * h, 128 * i:128 * i + 128], ctx_T[:, S * b:S * b + S],
                                            wv_sb, start=True, stop=True)
                last.then_inc(vproj_done, 1)

            pe.wait_ge(in_pk, 16)
            pe.wait_ge(in_ctx[0], 16)
            proj(0, 0, wk_sb, ctx_T, 0)
            pe.wait_ge(in_pv, 16)
            vproj(0)
            turn(0)
            pe.wait_ge(xnT_sb, 1)
            proj(1, 2, wq_sb, xn_T, 0)
            pe.wait_ge(in_ctx[1], 16)
            proj(2, 4, wk_sb, ctx_T, 1)
            vproj(1)
            turn(1)
            pe.wait_ge(xnT_sb, 2)
            proj(3, 5, wq_sb, xn_T, 1)

            def rows64(j):
                return slice(64 * j, 64 * j + 64)

            def scores(t, c, h):
                b = both(t, c)
                u = c % 2
                if h == 0:
                    pe.wait_ge(kst_done, b + 1)
                    pe.wait_ge(qst_done, b + 1)
                after(pe, max_done, 2 * b + h)
                for i in range(4):
                    for j in range(2):
                        last = nc.tensor.matmul(ps_s[:, j, i, :], q_st[u][rows64(j), 4 * h + i, :],
                                                k_st[u][rows64(j), 4 * h + i, :], start=True, stop=True)
                last.then_inc(s_done, 1)

            def scores_T(t, c, h):
                b = both(t, c)
                u = c % 2
                if h == 0:
                    pe.wait_ge(row_in[u], 32 * (t + c // 2 + 1))
                after(pe, p_done, 2 * b + h)
                for i in range(4):
                    for j in range(2):
                        last = nc.tensor.matmul(ps_t[:, j, i, :], k_st[u][rows64(j), 4 * h + i, :],
                                                q_st[u][rows64(j), 4 * h + i, :], start=True, stop=True)
                last.then_inc(t_done, 1)

            def minus_T(t, c, b):
                pe.wait_ge(nm_done, both(t, c) + 1)
                nc.tensor.transpose(ps_nm, nm[c % 2][:, :, :, :].rearrange("p j a g -> p (j a g)"), id_bf[:, :])\
                    .then_inc(nmT_done, 1)

            def products(t, c, h, between=None):
                b = both(t, c)
                pe.wait_ge(p_done, 2 * b + h + 1)
                if h == 0:
                    pe.wait_ge(v_in[c % 2], 16 * (t + c // 2 + 1))
                if h == 0:
                    after(pe, on_done, b)
                for i in range(8):
                    if h == 0 and i == 4 and between:
                        between()
                    head = 8 * h + i
                    last = nc.tensor.matmul(ps_o[h][:, VW * i:VW * i + WIN], prob[h][:, head % 2, head // 2 % 4, :],
                                            v_st[c % 2][:, VW * head:VW * head + WIN], start=True, stop=True)
                last.then_inc(av_done, 1)

            def out_T(t, c):
                b = both(t, c)
                pe.wait_ge(on_done, b + 1)
                after(pe, x1_done, b)
                nc.tensor.transpose(ps_oT, o_n[c % 2][:, :], id_sb).then_inc(oT_done, 1)

            def out_proj(t, c):
                pe.wait_ge(oT_sb, both(t, c) + 1)
                nc.tensor.matmul(ps_op, o_T[c % 2][:, :], wo_sb, start=True, stop=True).then_inc(op_done, 1)

            def turn_x(t, c, b):
                pe.wait_ge(xf_done, both(t, c) + 1)
                if b + 3 < B:
                    pe.wait_ge(nmT_sb, both(t, c) + 4)
                nc.tensor.transpose(ps_xT, xf[c % 2][:, :], id_sb).then_inc(xT_done, 1)

            scores(0, 0, 0)
            scores(0, 0, 1)
            pe.wait_ge(id_ready, 1)
            minus_T(0, 0, 0)
            scores(0, 1, 0)

            def step(t, c, b):
                scores_T(t, c, 0)
                if b + 1 < B:
                    scores(t, c + 1, 1)
                if b >= 1:
                    products(t, c - 1, 1)
                scores_T(t, c, 1)
                if b + 1 < B:
                    minus_T(t, c + 1, b + 1)
                if b >= 1:
                    out_T(t, c - 1)
                products(t, c, 0, (lambda: out_proj(t, c - 1)) if b >= 1 else None)
                if b >= 2:
                    turn_x(t, c - 2, b - 2)
                if b + 2 < B:
                    scores(t, c + 2, 0)
            attention_steps(step)(pe)
            products(B // 2 - 1, 1, 1)
            out_T(B // 2 - 1, 1)
            turn_x(B // 2 - 1, 0, B - 2)
            out_proj(B // 2 - 1, 1)

            def logits(b):
                pe.wait_ge(xT_sb, b + 1)
                return nc.tensor.matmul(ps_lg[:, E * b:E * b + E], xf_T[:, S * b:S * b + S], gb[:, 0, :],
                                        start=True, stop=True)

            pe.wait_ge(x1_done, B)
            pe.wait_ge(filled_1, 1)
            pe.wait_ge(gb_done, 2)
            nc.tensor.matmul(ps_gs, ones_mat[:, :], gb[:, :, :], start=True, stop=True)
            for b in range(B - 1):
                logits(b)
            turn_x(B // 2 - 1, 1, B - 1)
            logits(B - 1).then_inc(lg_mm, 1)
            pe.wait_ge(xlo_done, B)

            def first(t, n):
                k = 4 * t + n
                u, ch = (n // 2) % 2, n % 2
                e = 2 * t + n // 2
                pe.wait_ge(w1l_done, e + 1)
                after(pe, gelu_done, k - 1)
                a = slice(512 * ch, 512 * ch + 512)
                for fh in range(FH):
                    w = slice(P * fh, P * fh + P)
                    for i, (l, r) in enumerate(((w1_lo, xf_hi), (w1_hi, xf_lo), (w1_hi, xf_hi))):
                        last = nc.tensor.matmul(ps[:, 2 * (n % 2) + fh, :], l[u][:, w], r[:, a],
                                                start=(i == 0), stop=(i == 2))
                last.then_inc(f1_done, 1)

            def second(t, n):
                k = 4 * t + n
                u = n // 2
                pe.wait_ge(gelu_done, k + 1)
                if n % 2 == 0:
                    pe.wait_ge(w2_in[u], 16 * (t + 1))
                after(pe, acc_done, k - 1)
                for i in range(4):
                    for fh in range(FH):
                        last = nc.tensor.matmul(ps[:, 4 + n % 2, 128 * i:128 * i + 128],
                                                h_sb[n % 2][:, fh, 128 * i:128 * i + 128], w2_sb[u][:, fh, :],
                                                start=(fh == 0), stop=(fh == FH - 1))
                last.then_inc(f2_done, 1)

            first(0, 0)
            for n in range(4):
                first(0, n + 1)
                second(0, n)
            with pe.Fori(1, E // 2 - 1) as t:
                for n in range(4):
                    first(t, n + 1)
                    second(t, n)
            for n in range(4):
                if n < 3:
                    first(E // 2 - 1, n + 1)
                second(E // 2 - 1, n)


def kernel(**inputs):
    import ml_dtypes
    import numpy as np
    import concourse.bacc as bacc
    from concourse.bass_utils import run_bass_kernel_spmd as run

    a = {k: np.asarray(v) for k, v in inputs.items()}
    head_major = lambda w: w.reshape(w.shape[0], G, 2, DK).transpose(0, 2, 3, 1).reshape(w.shape[0], D)
    arrays = {
        "x": a["x"],
        "ctxT": a["ctx_1024"].reshape(B * S, D).T,
        "pack_k": np.concatenate([head_major(a["L0_xattn_Wk"]), head_major(a["L0_xattn_Wq"]),
                                  np.eye(P, dtype=np.float32), head_major(a["L0_xattn_bk"][None, :]).T,
                                  head_major(a["L0_xattn_bq"][None, :]).T, a["L0_ffn_ln_gamma"][:, None],
                                  a["L0_ffn_ln_beta"][:, None], a["L0_ffn_gate_w"].T], axis=1),
        "pack_v": np.concatenate([a["L0_xattn_Wv"], a["L0_xattn_Wo"]], axis=1),
        "row": np.concatenate([a["L0_xattn_bv"], a["L0_xattn_bo"],
                               np.tril(np.ones((E, E), np.float32), -1).reshape(-1)])[None, :],
        "w1T": a["L0_ffn_w1"].transpose(0, 2, 1),
        "w2T": a["L0_ffn_w2"].transpose(0, 2, 1).reshape(E, FH, P, D).transpose(0, 2, 1, 3),
        "ones": np.ones((2, B * G * S), np.float32).astype(ml_dtypes.bfloat16),
    }
    arrays = {k: np.ascontiguousarray(v) for k, v in arrays.items()}
    nc = bacc.Bacc("TRN2", target_bir_lowering=False, num_devices=1)
    args = {k: nc.dram_tensor(f"in_{k}", v.shape, mybir.dt.from_np(v.dtype), kind="ExternalInput").ap()
            for k, v in arrays.items()}
    out = nc.dram_tensor("out", (B, S, D), F32, kind="ExternalOutput").ap()
    build(nc, out=out, **args)
    r = run(nc, [{f"in_{k}": v for k, v in arrays.items()}], core_ids=[0])
    return r.results[0]["out"]
```

```python
from contextlib import ExitStack

import concourse.bass as bass
from concourse import mybir

F32 = mybir.dt.float32
F32R = mybir.dt.float32r
BF16 = mybir.dt.bfloat16
I32 = mybir.dt.int32
ALU = mybir.AluOpType
ACT = mybir.ActivationFunctionType
AX_X = mybir.AxisListType.X

P = 128
B, S, D = 8, 128, 128
H, DK = 16, 8
G = H // 2
E, F = 8, 256
FH = F // P
EPS = 1e-5
POOL_HI, POOL_MID, POOL_K, POOL_K1 = 2, 4, 4, (3, 5)
TWO_ONES = 0x3F803F80
SEGS = 6
K_SEG_PART = (0, 1, 2, 0, 1, 0)
Q_SEG_PART = (0, 0, 0, 1, 1, 2)
VW = DK + 1
WIN = 128
VCOLS = H * VW + WIN - VW
HALF = 4
CH = 2
CB = B // CH
N = CB * S
UNITS = E * CH


def build(nc, x, ctxT, pack_k, pack_v, row, w1T, w2T, comb_d, out):
    with ExitStack() as ctx:
        def sb(name, shape, dt=F32):
            return ctx.enter_context(nc.sbuf_tensor(name, shape, dt))

        def sem(name):
            return ctx.enter_context(nc.semaphore(name))

        x_all = sb("x_all", [P, B, D])
        ctx_T = sb("ctx_T", [P, B * S])
        xn = sb("xn", [P, B, D])
        xn_T = sb("xn_T", [P, B * S])
        k_part = sb("k_part", [P, 3, B * S], BF16)
        q_part = sb("q_part", [P, 3, B * S], BF16)
        rest = sb("rest", [P, 4, HALF * S])
        h_sb = [rest[:, FH * u:FH * (u + 1), :] for u in range(2)]
        h_hi = [sb(f"h_hi{u}", [P, FH, N], F32R) for u in range(2)]
        h_lo = [sb(f"h_lo{u}", [P, FH, N], F32R) for u in range(2)]
        pk = sb("pk", [P, 3 * D + 4 + E])
        wk_sb, wq_sb, id_sb = (pk[:, D * i:D * i + D] for i in range(3))
        bk_sb, bq_sb, gam_sb, bet_sb = (pk[:, 3 * D + i:3 * D + i + 1] for i in range(4))
        gate_sb = pk[:, 3 * D + 4:3 * D + 4 + E]
        pv = sb("pv", [P, 2 * D])
        wv_sb, wo_sb = pv[:, 0:D], pv[:, D:2 * D]
        rw = sb("rw", [P, 2 * D + E * E])
        bv_sb, bo_sb = rw[:, 0:D], rw[:, D:2 * D]
        low_sb = rw[:, 2 * D:2 * D + E * E]
        id_bf = sb("id_bf", [P, P], BF16)
        ones_mat = sb("ones_mat", [P, P])
        stats1 = sb("stats1", [P, B, 6])
        mv1 = sb("mv1", [P, B, 2])
        consts = sb("consts", [P, 3, B])
        warm = sb("warm", [P, 1])
        rs1 = sb("rs1", [P, 2, B])
        k_res = sb("k_res", [P, G, B, S], BF16)
        q_res = sb("q_res", [P, G, B, S], BF16)
        cb = k_res[:, :, :, :].rearrange("p g b n -> p (g b n)").bitcast(F32).rearrange("p (e n) -> p e n", n=N)
        v_res = sb("v_res", [P, B, VCOLS])
        k_st = [sb(f"k_st{u}", [P, G, S], BF16) for u in range(2)]
        q_st = [sb(f"q_st{u}", [P, G, S], BF16) for u in range(2)]
        mx = [sb(f"mx{u}", [P, 2, G]) for u in range(2)]
        nm = [sb(f"nm{u}", [P, 2, 2, G], BF16) for u in range(2)]
        nm_T = [sb(f"nm_T{u}", [4 * G, S], BF16) for u in range(2)]
        prob = [sb(f"prob{h}", [P, 2, G // 2, S]) for h in range(2)]
        rden = sb("rden", [P, 2, H // 2])
        o_n = [sb(f"o_n{u}", [P, D]) for u in range(2)]
        o_T = [sb(f"o_T{u}", [P, S]) for u in range(2)]
        stats2 = [sb(f"stats2{u}", [P, 6]) for u in range(2)]
        mv2 = [sb(f"mv2{u}", [P, 2]) for u in range(2)]
        rs2 = [sb(f"rs2{u}", [P, 4, 1]) for u in range(2)]
        xf = [sb(f"xf{u}", [P, D]) for u in range(2)]
        xf_T = sb("xf_T", [P, B * S])
        stats3 = sb("stats3", [P, B, 6])
        mv3 = sb("mv3", [P, B, 2])
        rs3 = sb("rs3", [P, 2, B])
        xf_hi = sb("xf_hi", [P, B * S], F32R)
        xf_lo = sb("xf_lo", [P, B * S], F32R)
        gb = sb("gb", [P, 2, E])
        lg = sb("lg", [P, 4, B, E])
        lmax, lsum, lrec = sb("lmax", [P, B]), sb("lsum", [P, B]), sb("lrec", [P, B])
        pr = sb("pr", [P, B, E])
        rk = sb("rk", [P, 2, B, E, E])
        rank = sb("rank", [P, B, E])
        comb = sb("comb", [P, CH, E, CB])
        comb_T = [sb(f"comb_T{ch}", [CB * E, S]) for ch in range(CH)]
        w1_raw, w2_raw = sb("w1_raw", [P, E, F]), sb("w2_raw", [P, E, FH, D])
        w1_hi, w1_lo = sb("w1_hi", [P, E, F], F32R), sb("w1_lo", [P, E, F], F32R)
        w2_hi, w2_lo = sb("w2_hi", [P, E, FH, D], F32R), sb("w2_lo", [P, E, FH, D], F32R)
        y_w = [sb(f"y_w{u}", [P, N]) for u in range(2)]
        y_T = sb("y_T", [P, CH, N])
        ps = ctx.enter_context(nc.psum_tensor("ps", [P, 8, 512], F32))
        ps_s = ps[:, 0:2, :].rearrange("p j (g n) -> p j g n", n=S)
        ps_t = ps[:, 2:4, :].rearrange("p j (g n) -> p j g n", n=S)
        ps_o = [ps[:, 4 + h, :] for h in range(2)]
        ps_a, ps_b = ps[:, 6, :], ps[:, 7, :]
        ps_nm = ps_a[0:4 * G, 0:S // 2].bitcast(BF16)
        ps_xT = ps_b[:, 384:512]
        ps_oT, ps_op = ps_b[:, 0:128], ps_b[:, 128:256]
        ps_lg = ps_a[:, 256:256 + B * E]
        ps_gs = ps_a[:, 384:384 + 2 * E]

        ps_cT = ps_a[0:CB * E, 0:S]
        ps_y = ps_b

        in_x = [sem(f"in_x{h}") for h in range(2)]
        in_ctx = [sem(f"in_ctx{h}") for h in range(2)]
        in_pk, in_pv, in_rw = sem("in_pk"), sem("in_pv"), sem("in_rw")
        filled_c, filled_k, filled_q, filled_v, filled_1 = sem("filled_c"), sem("filled_k"), sem("filled_q"), sem("filled_v"), sem("filled_1")
        id_ready, warm_done = sem("id_ready"), sem("warm_done")
        st1_done, mv1_done, rstd1_done, xn_done = sem("st1_done"), sem("mv1_done"), sem("rstd1_done"), sem("xn_done")
        pool_step = sem("pool_step")
        xnT_done, xnT_sb = sem("xnT_done"), sem("xnT_sb")
        proj_done = [sem(f"proj{n}_done") for n in range(4)]
        hi_done = [sem(f"hi{n}_done") for n in range(4)]
        rest_done = [sem(f"rest{n}_done") for n in range(4)]
        mid_done = [sem(f"mid{n}_done") for n in range(4)]
        lo_done = [sem(f"lo{n}_done") for n in range(4)]
        stack_k = [sem(f"stack_k{h}") for h in range(2)]
        stack_q = [sem(f"stack_q{h}") for h in range(2)]
        stack_qp, stack_kp = sem("stack_qp"), [sem(f"stack_kp{h}") for h in range(2)]
        vproj_done, v_done = sem("vproj_done"), sem("v_done")
        kst_done, qst_done = sem("kst_done"), sem("qst_done")
        row_in = [sem(f"row_in{u}") for u in range(2)]
        s_done, max_done, nmh_done, nm_done, nmT_done, nmT_sb = (
            sem(n) for n in ("s_done", "max_done", "nmh_done", "nm_done", "nmT_done", "nmT_sb"))
        t_done, p_done, av_done, rden_done, on_done = (
            sem(n) for n in ("t_done", "p_done", "av_done", "rden_done", "on_done"))
        oT_done, oT_sb, op_done, x1_done, st2_done, mv2_done, rstd2_done, xf_done, st3_done = (
            sem(n) for n in ("oT_done", "oT_sb", "op_done", "x1_done", "st2_done", "mv2_done", "rstd2_done",
                             "xf_done", "st3_done"))
        xT_done, xT_sb, xhi_done, xlo_done, xb_done = sem("xT_done"), sem("xT_sb"), sem("xhi_done"), sem("xlo_done"), sem("xb_done")
        gb_done = sem("gb_done")
        rank_done = sem("rank_done")
        mv3_done, rstd3_done, lg_mm, gate_step, lexp_done, comb_done = (
            sem(n) for n in ("mv3_done", "rstd3_done", "lg_mm", "gate_step", "lexp_done", "comb_done"))
        w1_in, w2_in, wh_done, w1_done, w2_done = (sem(n) for n in ("w1_in", "w2_in", "wh_done", "w1_done", "w2_done"))
        cT_done, cT_sb, comb_out = sem("cT_done"), sem("cT_sb"), sem("comb_out")
        cb_in = sem("cb_in")
        f1_done, gelu_done, hhi_done, hlo_done, f2_done, yw_done, yT_done, y_done, acc_done, filled_y = (
            sem(n) for n in ("f1_done", "gelu_done", "hhi_done", "hlo_done", "f2_done", "yw_done", "yT_done",
                             "y_done", "acc_done", "filled_y"))
        out_done = sem("out_done")

        block = ctx.enter_context(nc.Block())

        def after(eng, s, n):
            if not isinstance(n, int) or n > 0:
                eng.wait_ge(s, n)

        def both(t, c):
            return 2 * t + c

        def attention_steps(step):
            def run(eng):
                for c in range(2):
                    step(0, c, c)
                with eng.Fori(1, B // 2 - 1) as t:
                    for c in range(2):
                        step(t, c, 2 + c)
                for c in range(2):
                    step(B // 2 - 1, c, B - 2 + c)
            return run

        GATE_STEPS, GATE_EXP = 14, 7


        @block.sync
        def _(sp):
            x_v = x.rearrange("b s d -> s b d")
            for h in range(2):
                a = slice(HALF * S * h, HALF * S * (h + 1))
                sp.dma_start(x_all[:, HALF * h:HALF * (h + 1), :], x_v[:, HALF * h:HALF * (h + 1), :])\
                    .then_inc(in_x[h], 16)
                if h == 0:
                    sp.dma_start(pk[:, :], pack_k).then_inc(in_pk, 16)
                sp.dma_start(ctx_T[:, a], ctxT[:, a]).then_inc(in_ctx[h], 16)
                if h == 0:
                    sp.dma_start(pv[:, :], pack_v).then_inc(in_pv, 16)
                    sp.dma_start(rw[:, :], row.broadcast_to([P, 2 * D + E * E])).then_inc(in_rw, 16)
            sp.dma_start(w1_raw[:, :, :], w1T.rearrange("e c f -> c e f")).then_inc(w1_in, 16)

            def segments(part, res, seg_part, h, hi, rst, lo, fill, done, others=(), wants=(0, 1, 2)):
                for want in wants:
                    s_ready = (hi, rst, lo)[want]
                    for s in range(SEGS):
                        if seg_part[s] == want and s not in others:
                            sp.wait_ge(s_ready, 1)
                            sp.wait_ge(fill, 1 + h)
                            dst = res[s:P:DK, :, HALF * h:HALF * (h + 1), :].rearrange("p g b n -> p g (b n)")
                            src = part[:, want, HALF * S * h:HALF * S * (h + 1)]
                            sp.dma_start(dst, src).then_inc(done, 16)

            segments(k_part, k_res, K_SEG_PART, 0, hi_done[0], mid_done[0], lo_done[0], filled_k, stack_k[0],
                     (POOL_K,))
            segments(q_part, q_res, Q_SEG_PART, 0, hi_done[1], mid_done[1], lo_done[1], filled_q, stack_q[0],
                     (POOL_HI, POOL_MID))

            def rows(t, c):
                u = c % 2
                sp.wait_ge(nmT_sb, both(t, c) + 1)
                sp.dma_start(q_st[u][6:P:32, :, :], nm_T[u][:, :]).then_inc(row_in[u], 16)

            sp.dma_start(w2_raw[:, :, :, :].rearrange("p e f n -> p e (f n)"),
                         w2T.rearrange("e p f n -> p e (f n)")).then_inc(w2_in, 16)
            segments(k_part, k_res, K_SEG_PART, 1, hi_done[2], mid_done[2], lo_done[2], filled_k, stack_k[1],
                     POOL_K1)
            rows(0, 0)
            segments(q_part, q_res, Q_SEG_PART, 1, hi_done[3], mid_done[3], lo_done[3], filled_q, stack_q[1], wants=(0,))
            rows(0, 1)
            segments(q_part, q_res, Q_SEG_PART, 1, hi_done[3], mid_done[3], lo_done[3], filled_q, stack_q[1], wants=(1, 2))
            def step(t, c, b):
                if 1 <= b < B - 1:
                    rows(t, c + 1)
            attention_steps(step)(sp)


            for ch in range(CH):
                sp.wait_ge(cT_sb, ch + 1)
                sp.dma_start(comb_d[ch], comb_T[ch][:, :]).then_inc(comb_out, 16)
                sp.wait_ge(comb_out, 16 * (ch + 1))
                for pair in range(E // 2):
                    n = E // 2 * ch + pair
                    after(sp, yw_done, 2 * (n - E // 2) + 2)
                    a = slice(2 * pair, 2 * pair + 2)
                    src = comb_d[ch:ch + 1, 2 * CB * pair:2 * CB * (pair + 1), :].rearrange("o r n -> o (r n)")
                    sp.dma_start(cb[:, a, :].rearrange("p e n -> p (e n)"),
                                 src.broadcast_to([P, 2 * N])).then_inc(cb_in, 16)
                    sp.wait_ge(cb_in, 16 * (n + 1))

            out_v = out.rearrange("b s d -> s b d")
            for n in range(2 * CH):
                sp.wait_ge(acc_done, n + 1)
                sp.dma_start(out_v[:, 2 * n:2 * n + 2, :], x_all[:, 2 * n:2 * n + 2, :]).then_inc(out_done, 16)
            sp.wait_ge(out_done, 16 * 2 * CH)

        @block.gpsimd
        def _(pool):
            steps = [0]

            def chained(ins, t=None):
                steps[0] += 1
                ins.then_inc(pool_step, 1)
                pool.wait_ge(pool_step, steps[0])

            for i, value in enumerate((EPS, -0.5, -1.0)):
                nc.gpsimd.memset(consts[:, i, :], value).then_inc(filled_c, 1)
            pool.wait_ge(filled_c, 3)
            nc.gpsimd.memset(q_res[:, :, 0:HALF, :].bitcast(I32), 0).then_inc(filled_q, 1)
            def inv_root(w, var, count):
                n = w.shape[2]
                count(nc.gpsimd.tensor_tensor(w[:, 0, :], var, consts[:, 0, 0:n], ALU.add))
                return nc.gpsimd.tensor_tensor(w[:, 1, :], w[:, 0, :], consts[:, 1, 0:n], ALU.pow)

            def half1(w, h):
                return w[:, :, HALF * h:HALF * (h + 1)]

            def root1(h):
                pool.wait_ge(mv1_done, HALF * (h + 1))
                inv_root(half1(rs1, h), mv1[:, HALF * h:HALF * (h + 1), 1], chained).then_inc(rstd1_done, 1)

            root1(0)
            nc.gpsimd.memset(v_res[:, 0:HALF, :], 1.0).then_inc(filled_v, 1)
            nc.gpsimd.memset(k_res[:, :, HALF:B, :].bitcast(I32), TWO_ONES).then_inc(filled_k, 1)

            def move(part, res, seg_part, h, s, part_ready, done):
                pool.wait_ge(part_ready, 1)
                nc.gpsimd.dma_start(res[s:P:DK, :, HALF * h:HALF * (h + 1), :].rearrange("p g b n -> p g (b n)"),
                                    part[:, seg_part[s], HALF * S * h:HALF * S * (h + 1)]).then_inc(done, 16)

            pool.wait_ge(filled_k, 2)
            move(k_part, k_res, K_SEG_PART, 0, POOL_K, mid_done[0], stack_kp[0])
            root1(1)
            move(q_part, q_res, Q_SEG_PART, 0, POOL_HI, hi_done[1], stack_qp)
            move(q_part, q_res, Q_SEG_PART, 0, POOL_MID, mid_done[1], stack_qp)
            nc.gpsimd.memset(q_res[:, :, HALF:B, :].bitcast(I32), 0).then_inc(filled_q, 1)
            nc.gpsimd.memset(v_res[:, HALF:B, :], 1.0).then_inc(filled_v, 1)
            for s in POOL_K1:
                move(k_part, k_res, K_SEG_PART, 1, s, hi_done[2], stack_kp[1])
            nc.gpsimd.memset(ones_mat[:, :], 1.0).then_inc(filled_1, 1)
            pool.wait_ge(xn_done, B)
            pool.wait_ge(in_rw, 16)
            nc.gpsimd.tensor_tensor(x_all[:, :, :], x_all[:, :, :],
                                    bo_sb.rearrange("p (o d) -> p o d", o=1).broadcast_to([P, B, D]),
                                    ALU.add).then_inc(xb_done, 1)

            nc.gpsimd.memset(y_T[:, :, :], 0.0).then_inc(filled_y, 1)

            def split(hi, lo, raw, n, done):
                nc.gpsimd.tensor_copy(hi, raw).then_inc(wh_done, 1)
                pool.wait_ge(wh_done, n)
                nc.gpsimd.tensor_tensor(lo, raw, hi, ALU.subtract).then_inc(done, 1)

            def split1(e):
                split(w1_hi[:, e, :], w1_lo[:, e, :], w1_raw[:, e, :], e + 1, w1_done)

            def split2(e):
                a = bass.ds(e, 1)
                split(w2_hi[:, a, :, :], w2_lo[:, a, :, :], w2_raw[:, a, :, :], e + (E + 1), w2_done)

            pool.wait_ge(w1_in, 16)
            for e in range(E):
                split1(e)
            pool.wait_ge(w2_in, 16)
            for e in range(E // 2):
                split2(e)

            base = steps[0]
            CHAIN2 = 3

            def root2(t, c):
                u = c % 2
                b = both(t, c)
                pool.wait_ge(mv2_done, b + 1)
                k = [0]

                def count(ins):
                    k[0] += 1
                    ins.then_inc(pool_step, 1)
                    pool.wait_ge(pool_step, b * CHAIN2 + (base + k[0]))
                count(inv_root(rs2[u], mv2[u][:, 1:2], count))
                count(nc.gpsimd.tensor_tensor(rs2[u][:, 2, :], mv2[u][:, 0:1], consts[:, 2, 0:1], ALU.mult))
                nc.gpsimd.tensor_tensor(rs2[u][:, 3, :], rs2[u][:, 2, :], rs2[u][:, 1, :], ALU.mult)\
                    .then_inc(rstd2_done, 1)
                assert k[0] == CHAIN2, k[0]

            def x_lo(t, c):
                b = both(t, c)
                pool.wait_ge(xT_sb, b + 1)
                nc.gpsimd.tensor_tensor(xf_lo[:, bass.ds(b * S, S)], xf_T[:, bass.ds(b * S, S)], xf_hi[:, bass.ds(b * S, S)],
                                        ALU.subtract).then_inc(xlo_done, 1)

            def root3(b0, b1):
                pool.wait_ge(mv3_done, b1)
                inv_root(rs3[:, :, b0:b1], mv3[:, b0:b1, 1], chained).then_inc(rstd3_done, 1)

            last = B // 2 - 1
            root2(0, 0)
            with pool.Fori(0, B // 4) as t:
                for c in range(1, 3):
                    split2(2 * t + (c + E // 2 - 1))
                    root2(t, c)
                    x_lo(t, c - 1)
            steps[0] = base + (B // 2 + 1) * CHAIN2
            root3(0, CB)
            base += 1
            root2(last, -1)
            x_lo(last, -2)
            root2(last, 0)
            x_lo(last, -1)
            root2(last, 1)
            steps[0] = base + B * CHAIN2
            x_lo(last, 0)
            root3(CB, B - 1)
            root3(B - 1, B)
            x_lo(last, 1)

            def add_up(t, u, ch):
                k = 2 * t + u
                pool.wait_ge(yw_done, k + 1)
                after(pool, yT_done, k)
                nc.gpsimd.tensor_tensor(y_T[:, ch, :], y_w[u][:, :], y_T[:, ch, :], ALU.add).then_inc(yT_done, 1)
            pool.wait_ge(filled_y, 1)
            for u in range(2):
                add_up(0, u, 0)
            for t0, t1, ch in ((1, E // 2, 0), (E // 2, UNITS // 2 - 1, 1)):
                with pool.Fori(t0, t1) as t:
                    for u in range(2):
                        add_up(t, u, ch)

        @block.scalar
        def _(act):
            def hi_part(n, bank, bias, part, h):
                act.wait_ge(proj_done[n], 1)
                nc.scalar.activation(part[:, 0, HALF * S * h:HALF * S * (h + 1)], ps[:, bank, :], ACT.Identity,
                                     bias=bias).then_inc(hi_done[n], 1)

            def mid_part(n, part, h):
                act.wait_ge(rest_done[n], 1)
                nc.scalar.activation(part[:, 1, HALF * S * h:HALF * S * (h + 1)], rest[:, n, :],
                                     ACT.Identity).then_inc(mid_done[n], 1)

            def xnT_copy(h):
                act.wait_ge(xnT_done, h + 1)
                nc.scalar.activation(xn_T[:, HALF * S * h:HALF * S * (h + 1)], ps[:, 1 + 4 * h, :],
                                     ACT.Identity).then_inc(xnT_sb, 1)

            act.wait_ge(filled_c, 1)
            nc.scalar.activation(warm[:, :], consts[:, 0, 0:1], ACT.Exp).then_inc(warm_done, 1)
            act.wait_ge(in_pk, 16)
            hi_part(0, 0, bk_sb, k_part, 0)
            xnT_copy(0)
            mid_part(0, k_part, 0)
            hi_part(1, 2, bq_sb, q_part, 0)
            mid_part(1, q_part, 0)

            def exps(t, c, h):
                b = both(t, c)
                act.wait_ge(t_done, 2 * b + h + 1)
                after(act, av_done, 2 * b + h - 1)
                nc.scalar.activation(prob[h][:, :, :, :], ps_t, ACT.Exp, scale=float(DK) ** -0.5)\
                    .then_inc(p_done, 1)

            def second_norm(t, c):
                b = both(t, c)
                act.wait_ge(rstd2_done, b + 1)
                nc.scalar.activation(xf[c % 2][:, :], x_all[:, b, :], ACT.Identity, scale=rs2[c % 2][:, 1, :],
                                     bias=rs2[c % 2][:, 3, :]).then_inc(xf_done, 1)

            def rows_out(t, c):
                b = both(t, c)
                act.wait_ge(nmT_done, b + 1)
                after(act, row_in[c % 2], 16 * (t + c // 2))
                nc.scalar.activation(nm_T[c % 2][:, :], ps_nm, ACT.Identity).then_inc(nmT_sb, 1)

            def oT_copy(t, c):
                b = both(t, c)
                act.wait_ge(oT_done, b + 1)
                nc.scalar.activation(o_T[c % 2][:, :], ps_oT, ACT.Identity).then_inc(oT_sb, 1)

            def x_T(t, c):
                b = both(t, c)
                act.wait_ge(xT_done, b + 1)
                nc.scalar.activation(xf_hi[:, bass.ds(b * S, S)], ps_xT, ACT.Identity).then_inc(xhi_done, 1)
                nc.scalar.activation(xf_T[:, bass.ds(b * S, S)], ps_xT, ACT.Identity).then_inc(xT_sb, 1)

            def exp_gate(ch):
                a = slice(CB * ch, CB * (ch + 1))
                act.wait_ge(gate_step, GATE_STEPS * ch + GATE_EXP)
                nc.scalar.activation(pr[:, a, :], lg[:, 0, a, :], ACT.Exp).then_inc(lexp_done, 1)

            hi_part(2, 4, bk_sb, k_part, 1)
            xnT_copy(1)
            mid_part(2, k_part, 1)
            hi_part(3, 5, bq_sb, q_part, 1)
            rows_out(0, 0)

            def step(t, c, b):
                exps(t, c, 0)
                if b == B - 1:
                    exp_gate(0)
                if b + 1 < B:
                    rows_out(t, c + 1)
                if b == 0:
                    mid_part(3, q_part, 1)
                if b == B - 1:
                    oT_copy(t, c - 1)
                exps(t, c, 1)
                if 1 <= b < B - 1:
                    oT_copy(t, c - 1)
                if b >= 2:
                    second_norm(t, c - 2)
                if b >= 2:
                    x_T(t, c - 2)
            attention_steps(step)(act)
            last = B // 2 - 1
            nc.scalar.activation(warm[:, :], consts[:, 0, 0:1], ACT.Gelu).then_inc(warm_done, 1)
            second_norm(last, 0)
            oT_copy(last, 1)

            def gelu(t, u):
                k = 2 * t + u
                act.wait_ge(f1_done, k + 1)
                after(act, hlo_done, k - 1)
                nc.scalar.activation(h_sb[u][:, :, :], ps[:, 2 * u:2 * u + 2, :], ACT.Gelu).then_inc(gelu_done, 1)

            def high(t, u):
                k = 2 * t + u
                act.wait_ge(gelu_done, k + 1)
                after(act, f2_done, k - 1)
                nc.scalar.activation(h_hi[u][:, :, :], h_sb[u][:, :, :], ACT.Copy).then_inc(hhi_done, 1)

            gelu(0, 0)
            high(0, 0)
            x_T(last, 0)
            gelu(0, 1)
            second_norm(last, 1)
            high(0, 1)
            x_T(last, 1)
            for u in range(2):
                gelu(1, u)
                high(1, u)
            exp_gate(1)
            nc.scalar.activation(warm[:, :], consts[:, 0, 0:1], ACT.Gelu).then_inc(warm_done, 1)
            with act.Fori(2, UNITS // 2) as t:
                for u in range(2):
                    gelu(t, u)
                    high(t, u)

        @block.vector
        def _(dve):
            nc.vector.memset(k_res[:, :, 0:HALF, :].bitcast(I32), TWO_ONES).then_inc(filled_k, 1)

            def stats(h):
                dve.wait_ge(in_x[h], 16)
                for b in range(HALF * h, HALF * (h + 1)):
                    nc.vector.bn_stats(stats1[:, b, :], x_all[:, b, :]).then_inc(st1_done, 1)
                for b in range(HALF * h, HALF * (h + 1)):
                    dve.wait_ge(st1_done, b + 1)
                    nc.vector.bn_aggr(mv1[:, b, :], stats1[:, b, :]).then_inc(mv1_done, 1)

            def normal(h):
                dve.wait_ge(rstd1_done, h + 1)
                for b in range(HALF * h, HALF * (h + 1)):
                    nc.vector.tensor_scalar(xn[:, b, :], x_all[:, b, :], mv1[:, b, 0:1], rs1[:, 1, b:b + 1],
                                            ALU.subtract, ALU.mult).then_inc(xn_done, 1)

            def second_part(n, bank, bias, part, h):
                dve.wait_ge(hi_done[n], 1)
                a = slice(HALF * S * h, HALF * S * (h + 1))
                nc.vector.scalar_tensor_tensor(out=rest[:, n, :], in0=ps[:, bank, :], scalar=bias,
                                               in1=part[:, 0, a], op0=ALU.add, op1=ALU.subtract)\
                    .then_inc(rest_done[n], 1)

            def third_part(n, part, h):
                dve.wait_ge(mid_done[n], 1)
                a = slice(HALF * S * h, HALF * S * (h + 1))
                nc.vector.tensor_tensor(part[:, 2, a], rest[:, n, :], part[:, 1, a], ALU.subtract)\
                    .then_inc(lo_done[n], 1)

            def values(h):
                dve.wait_ge(vproj_done, h + 1)
                dve.wait_ge(filled_v, h + 1)
                dve.wait_ge(in_rw, 16)
                nc.vector.tensor_tensor(
                    v_res[:, HALF * h:HALF * (h + 1), 0:H * VW].rearrange("p b (h e) -> p b h e", e=VW)[:, :, :, 0:DK],
                    ps[:, 3 + 4 * h, :].rearrange("p (b h d) -> p b h d", b=HALF, d=DK),
                    bv_sb.rearrange("p (o h d) -> p o h d", o=1, d=DK).broadcast_to([P, HALF, H, DK]),
                    ALU.add).then_inc(v_done, 1)

            def stack_copy(t, c, h):
                after(dve, t_done, 2 * (both(t, c) - 2) + h + 1)
                a = slice(4 * h, 4 * h + 4)
                nc.vector.tensor_copy(k_st[c % 2][:, a, :], k_res[:, a, both(t, c), :]).then_inc(kst_done, 1)
                nc.vector.tensor_copy(q_st[c % 2][:, a, :], q_res[:, a, both(t, c), :]).then_inc(qst_done, 1)

            stats(0)
            normal(0)
            second_part(0, 0, bk_sb, k_part, 0)
            stats(1)
            third_part(0, k_part, 0)
            dve.wait_ge(in_pk, 16)
            nc.vector.tensor_copy(id_bf[:, :], id_sb).then_inc(id_ready, 1)
            second_part(1, 2, bq_sb, q_part, 0)
            third_part(1, q_part, 0)
            normal(1)
            values(0)
            second_part(2, 4, bk_sb, k_part, 1)
            dve.wait_ge(stack_k[0], 16 * (SEGS - 1))
            dve.wait_ge(stack_kp[0], 16)
            dve.wait_ge(stack_q[0], 16 * (SEGS - 2))
            dve.wait_ge(stack_qp, 16 * 2)
            stack_copy(0, 0, 0)
            stack_copy(0, 0, 1)

            def maxima(t, c, h, banks=ps_s):
                b = both(t, c)
                dve.wait_ge(s_done, 2 * b + h + 1)
                after(dve, nm_done, b - 1)
                nc.vector.tensor_reduce(mx[c % 2][:, :, 4 * h:4 * h + 4], banks, AX_X, ALU.max)\
                    .then_inc(max_done, 1)

            def minus(t, c):
                b = both(t, c)
                u = c % 2
                dve.wait_ge(max_done, 2 * b + 2)
                after(dve, nmT_done, b - 1)
                nc.vector.tensor_scalar(nm[u][:, :, 0, :], mx[u][:, :, :], -1.0, None, ALU.mult).then_inc(nmh_done, 1)
                dve.wait_ge(nmh_done, b + 1)
                nc.vector.scalar_tensor_tensor(out=nm[u][:, :, 1, :], in0=mx[u][:, :, :], scalar=-1.0,
                                               in1=nm[u][:, :, 0, :], op0=ALU.mult, op1=ALU.subtract)\
                    .then_inc(nm_done, 1)

            def norm(t, c):
                b = both(t, c)
                dve.wait_ge(av_done, 2 * b + 2)
                acc = ps[:, 4:6, 0:8 * VW].rearrange("p a (h e) -> p a h e", e=VW)
                after(dve, on_done, b)
                nc.vector.reciprocal(rden[:, :, :], acc[:, :, :, DK]).then_inc(rden_done, 1)
                dve.wait_ge(rden_done, b + 1)
                nc.vector.tensor_tensor(
                    o_n[c % 2][:, :].rearrange("p (a h d) -> p a h d", a=2, d=DK), acc[:, :, :, 0:DK],
                    rden[:, :, :].rearrange("p a (h o) -> p a h o", o=1).broadcast_to([P, 2, H // 2, DK]), ALU.mult)\
                    .then_inc(on_done, 1)

            def residual(t, c):
                b = both(t, c)
                u = c % 2
                dve.wait_ge(op_done, b + 1)
                if c < 2 and isinstance(t, int):
                    dve.wait_ge(xb_done, 1)
                nc.vector.tensor_tensor(x_all[:, b, :], ps_op, x_all[:, b, :], ALU.add).then_inc(x1_done, 1)

            def stats_x1(t, c):
                b = both(t, c)
                u = c % 2
                dve.wait_ge(xb_done, 1)
                dve.wait_ge(x1_done, b + 1)
                nc.vector.bn_stats(stats2[u][:, :], x_all[:, b, :]).then_inc(st2_done, 1)
                dve.wait_ge(xb_done, 1)
                dve.wait_ge(st2_done, b + 1)
                nc.vector.bn_aggr(mv2[u][:, :], stats2[u][:, :]).then_inc(mv2_done, 1)

            def stats_xf(t, c):
                b = both(t, c)
                dve.wait_ge(xb_done, 1)
                dve.wait_ge(xf_done, b + 1)
                nc.vector.bn_stats(stats3[:, b, :], xf[c % 2][:, :]).then_inc(st3_done, 1)

            def aggregate(b0, b1):
                for b in range(b0, b1):
                    dve.wait_ge(st3_done, b + 1)
                    nc.vector.bn_aggr(mv3[:, b, :], stats3[:, b, :]).then_inc(mv3_done, 1)

            steps = [0]

            def chained(ins):
                steps[0] += 1
                ins.then_inc(gate_step, 1)
                dve.wait_ge(gate_step, steps[0])

            def over_e(a):
                return a.rearrange("p (b o) -> p b o", o=1).broadcast_to([P, CB, E])

            def over_b(a):
                return a.rearrange("p (o e) -> p o e", o=1).broadcast_to([P, CB, E])

            def gate_logits(ch):
                a = slice(CB * ch, CB * (ch + 1))
                dve.wait_ge(mv3_done, CB * (ch + 1))
                dve.wait_ge(lg_mm, ch + 1)
                chained(nc.vector.tensor_tensor(lg[:, 1, a, :], mv3[:, a, 0:1].broadcast_to([P, CB, E]),
                                                over_b(ps_gs[:, 0:E]), ALU.mult))
                chained(nc.vector.tensor_tensor(lg[:, 2, a, :], ps_lg.rearrange("p (b e) -> p b e", e=E)[:, a, :],
                                                lg[:, 1, a, :], ALU.subtract))
                dve.wait_ge(rstd3_done, 1 + 2 * ch)
                chained(nc.vector.tensor_tensor(lg[:, 1, a, :], lg[:, 2, a, :], over_e(rs3[:, 1, a]), ALU.mult))
                chained(nc.vector.tensor_tensor(lg[:, 2, a, :], lg[:, 1, a, :], over_b(ps_gs[:, E:2 * E]), ALU.add))
                chained(nc.vector.tensor_reduce(lmax[:, a], lg[:, 2, a, :], AX_X, ALU.max))
                chained(nc.vector.tensor_tensor(lg[:, 3, a, :], lg[:, 2, a, :], over_e(lmax[:, a]), ALU.subtract))
                chained(nc.vector.tensor_copy(lg[:, 0, a, :], lg[:, 3, a, :]))
                assert steps[0] == GATE_STEPS * ch + GATE_EXP

            def gate_weights(ch, stage):
                a = slice(CB * ch, CB * (ch + 1))
                prob_e = lg[:, 1, a, :]
                eq = rk[:, 1, a, :, :].rearrange("p b a c -> p b (a c)")
                gt = rk[:, 0, a, :, :].rearrange("p b a c -> p b (a c)")
                if stage == 0:
                    dve.wait_ge(lexp_done, ch + 1)
                    chained(nc.vector.tensor_reduce(lsum[:, a], pr[:, a, :], AX_X, ALU.add))
                    chained(nc.vector.reciprocal(lrec[:, a], lsum[:, a]))
                    chained(nc.vector.tensor_tensor(prob_e, pr[:, a, :], over_e(lrec[:, a]), ALU.mult))
                if stage == 1:
                    mine = prob_e.rearrange("p b (e o) -> p b e o", o=1).broadcast_to([P, CB, E, E])
                    their = prob_e.rearrange("p b (o e) -> p b o e", o=1).broadcast_to([P, CB, E, E])
                    nc.vector.tensor_tensor(rk[:, 0, a, :, :], their, mine, ALU.is_gt).then_inc(gate_step, 1)
                    steps[0] += 1
                    chained(nc.vector.tensor_tensor(rk[:, 1, a, :, :], their, mine, ALU.is_equal))
                    low_b = low_sb.rearrange("p (o n) -> p o n", o=1).broadcast_to([P, CB, E * E])
                    chained(nc.vector.tensor_tensor(eq, eq, low_b, ALU.mult))
                if stage == 2:
                    chained(nc.vector.tensor_tensor(gt, gt, eq, ALU.add))
                    nc.vector.tensor_reduce(rank[:, a, :], rk[:, 0, a, :, :], AX_X, ALU.add).then_inc(rank_done, 1)
                    dve.wait_ge(rank_done, ch + 1)
                    nc.vector.scalar_tensor_tensor(out=comb[:, ch, :, :].rearrange("p e b -> p b e"),
                                                   in0=rank[:, a, :], scalar=1.5, in1=prob_e,
                                                   op0=ALU.is_lt, op1=ALU.mult).then_inc(comb_done, 1)
                    assert steps[0] == GATE_STEPS * (ch + 1)

            def comb_out_copy(ch):
                dve.wait_ge(cT_done, ch + 1)
                nc.vector.tensor_copy(comb_T[ch][:, :], ps_cT).then_inc(cT_sb, 1)

            maxima(0, 0, 0)
            maxima(0, 0, 1, ps_t)
            minus(0, 0)
            stack_copy(0, 1, 0)
            stack_copy(0, 1, 1)
            third_part(2, k_part, 1)
            maxima(0, 1, 0)
            maxima(0, 1, 1)
            minus(0, 1)
            nc.vector.tensor_scalar(gb[:, 0, :], gate_sb, gam_sb, None, ALU.mult).then_inc(gb_done, 1)
            nc.vector.tensor_scalar(gb[:, 1, :], gate_sb, bet_sb, None, ALU.mult).then_inc(gb_done, 1)
            second_part(3, 5, bq_sb, q_part, 1)

            def step(t, c, b):
                if b == B - 2:
                    aggregate(0, CB)
                if b + 2 < B:
                    if b == 1:
                        dve.wait_ge(stack_k[1], 16 * (SEGS - len(POOL_K1)))
                        dve.wait_ge(stack_kp[1], 16 * len(POOL_K1))
                        dve.wait_ge(stack_q[1], 16 * SEGS)
                    stack_copy(t, c + 2, 0)
                if b >= 1:
                    norm(t, c - 1)
                if b == B - 1:
                    gate_weights(0, 0)
                    gate_weights(0, 1)
                if b + 2 < B:
                    stack_copy(t, c + 2, 1)
                    if b == 0:
                        third_part(3, q_part, 1)
                    maxima(t, c + 2, 0)
                    if b == 0:
                        values(1)
                if b >= 1:
                    residual(t, c - 1)
                if b == B - 2:
                    gate_logits(0)
                if b + 2 < B:
                    maxima(t, c + 2, 1)
                    minus(t, c + 2)
                if b >= 1:
                    stats_x1(t, c - 1)
                if b == B - 1:
                    gate_weights(0, 2)
                if b >= 2:
                    stats_xf(t, c - 2)
            attention_steps(step)(dve)
            last = B // 2 - 1
            norm(last, 1)
            comb_out_copy(0)
            stats_xf(last, 0)
            aggregate(CB, B - 1)
            residual(last, 1)
            stats_x1(last, 1)

            def low(t, u):
                k = 2 * t + u
                dve.wait_ge(hhi_done, k + 1)
                after(dve, f2_done, k - 1)
                nc.vector.tensor_tensor(h_lo[u][:, :, :], h_sb[u][:, :, :], h_hi[u][:, :, :], ALU.subtract)\
                    .then_inc(hlo_done, 1)

            def weigh(t, u, ch):
                k = 2 * t + u
                if u == 0:
                    dve.wait_ge(cb_in, 16 * t + 16)
                dve.wait_ge(f2_done, k + 1)
                after(dve, yT_done, k - 1)
                nc.vector.tensor_tensor(y_w[u][:, :], ps[:, 4 + u, :],
                                        cb[:, bass.ds(k - E * ch, 1), :].rearrange("p e n -> p (e n)"), ALU.mult)\
                    .then_inc(yw_done, 1)

            def add_out(ch):
                dve.wait_ge(y_done, ch + 1)
                for h in range(2):
                    a = slice(CB * ch + 2 * h, CB * ch + 2 * h + 2)
                    nc.vector.tensor_tensor(x_all[:, a, :], ps_y[:, 2 * D * h:2 * D * (h + 1)].rearrange(
                        "p (b d) -> p b d", d=D), x_all[:, a, :], ALU.add).then_inc(acc_done, 1)

            low(0, 0)
            stats_xf(last, 1)
            aggregate(B - 1, B)
            low(0, 1)
            for k in range(2, 12):
                weigh(k // 2 - 1, k % 2, (k - 2) // E)
                if k == 8:
                    comb_out_copy(1)
                low(k // 2, k % 2)
                if k == 2:
                    gate_logits(1)
                if k in (4, 5, 6):
                    gate_weights(1, k - 4)
            add_out(0)
            with dve.Fori(6, UNITS // 2) as t:
                for u in range(2):
                    weigh(t - 1, u, 1)
                    low(t, u)
            for u in range(2):
                weigh(UNITS // 2 - 1, u, 1)
            add_out(1)

        @block.tensor
        def _(pe):
            def proj(n, bank, w, src, h):
                nc.tensor.matmul(ps[:, bank, :], w, src[:, HALF * S * h:HALF * S * (h + 1)],
                                 start=True, stop=True).then_inc(proj_done[n], 1)

            def turn(h):
                for b in range(HALF * h, HALF * (h + 1)):
                    pe.wait_ge(xn_done, b + 1)
                    i = b % HALF
                    last = nc.tensor.transpose(ps[:, 1 + 4 * h, 128 * i:128 * i + 128], xn[:, b, :], id_sb)
                last.then_inc(xnT_done, 1)

            def vproj(h):
                for b in range(HALF * h, HALF * (h + 1)):
                    i = b % HALF
                    last = nc.tensor.matmul(ps[:, 3 + 4 * h, 128 * i:128 * i + 128], ctx_T[:, S * b:S * b + S],
                                            wv_sb, start=True, stop=True)
                last.then_inc(vproj_done, 1)

            pe.wait_ge(in_pk, 16)
            pe.wait_ge(in_ctx[0], 16)
            proj(0, 0, wk_sb, ctx_T, 0)
            turn(0)
            pe.wait_ge(xnT_sb, 1)
            proj(1, 2, wq_sb, xn_T, 0)
            pe.wait_ge(in_pv, 16)
            vproj(0)
            pe.wait_ge(in_ctx[1], 16)
            proj(2, 4, wk_sb, ctx_T, 1)
            vproj(1)
            turn(1)

            def rows64(j):
                return slice(64 * j, 64 * j + 64)

            def scores(t, c, h, banks=ps_s):
                b = both(t, c)
                u = c % 2
                pe.wait_ge(kst_done, 2 * b + h + 1)
                pe.wait_ge(qst_done, 2 * b + h + 1)
                if banks is ps_s:
                    after(pe, max_done, 1 if isinstance(b, int) and (b, h) == (1, 0) else 2 * b + h)
                for i in range(4):
                    for j in range(2):
                        last = nc.tensor.matmul(banks[:, j, i, :], q_st[u][rows64(j), 4 * h + i, :],
                                                k_st[u][rows64(j), 4 * h + i, :], start=True, stop=True)
                last.then_inc(s_done, 1)

            def scores_T(t, c, h):
                b = both(t, c)
                u = c % 2
                if h == 0:
                    pe.wait_ge(row_in[u], 16 * (t + c // 2 + 1))
                after(pe, p_done, 2 * b + h)
                for i in range(4):
                    for j in range(2):
                        last = nc.tensor.matmul(ps_t[:, j, i, :], k_st[u][rows64(j), 4 * h + i, :],
                                                q_st[u][rows64(j), 4 * h + i, :], start=True, stop=True)
                last.then_inc(t_done, 1)

            def minus_T(t, c):
                pe.wait_ge(nm_done, both(t, c) + 1)
                nc.tensor.transpose(ps_nm, nm[c % 2][:, :, :, :].rearrange("p j a g -> p (j a g)"), id_bf[:, :])\
                    .then_inc(nmT_done, 1)

            def products(t, c, h, at=None, between=None):
                b = both(t, c)
                pe.wait_ge(p_done, 2 * b + h + 1)
                if isinstance(t, int) and h == 0:
                    pe.wait_ge(v_done, 1 if b < HALF else 2)
                if h == 0:
                    after(pe, on_done, b)
                for i in range(8):
                    if i == at:
                        between()
                    head = 8 * h + i
                    last = nc.tensor.matmul(ps_o[h][:, VW * i:VW * i + WIN], prob[h][:, head % 2, head // 2 % 4, :],
                                            v_res[:, both(t, c), VW * head:VW * head + WIN], start=True, stop=True)
                last.then_inc(av_done, 1)

            def out_T(t, c):
                b = both(t, c)
                pe.wait_ge(on_done, b + 1)
                after(pe, x1_done, b)
                nc.tensor.transpose(ps_oT, o_n[c % 2][:, :], id_sb).then_inc(oT_done, 1)

            def out_proj(t, c):
                pe.wait_ge(oT_sb, both(t, c) + 1)
                nc.tensor.matmul(ps_op, o_T[c % 2][:, :], wo_sb, start=True, stop=True).then_inc(op_done, 1)

            def turn_x(t, c, ahead):
                pe.wait_ge(xf_done, both(t, c) + 1)
                pe.wait_ge(x1_done, both(t, c) + ahead)
                nc.tensor.transpose(ps_xT, xf[c % 2][:, :], id_sb).then_inc(xT_done, 1)

            def gate_products(b0, b1):
                if b0 == 0:
                    pe.wait_ge(nmT_sb, B)
                    pe.wait_ge(filled_1, 1)
                    pe.wait_ge(gb_done, 2)
                    nc.tensor.matmul(ps_gs, ones_mat[:, :], gb[:, :, :], start=True, stop=True)
                for b in range(b0, b1):
                    pe.wait_ge(xT_sb, b + 1)
                    last = nc.tensor.matmul(ps_lg[:, E * b:E * b + E], xf_T[:, S * b:S * b + S], gb[:, 0, :],
                                            start=True, stop=True)
                return last

            def comb_turn(ch):
                pe.wait_ge(comb_done, ch + 1)
                nc.tensor.transpose(ps_cT, comb[:, ch, :, :].rearrange("p e b -> p (e b)"), id_sb)\
                    .then_inc(cT_done, 1)

            scores(0, 0, 0)
            pe.wait_ge(v_done, 1)
            scores(0, 0, 1, ps_t)
            pe.wait_ge(xnT_sb, 2)
            proj(3, 5, wq_sb, xn_T, 1)
            pe.wait_ge(id_ready, 1)
            minus_T(0, 0)
            scores(0, 1, 0)
            scores(0, 1, 1)

            def step(t, c, b):
                scores_T(t, c, 0)
                if b == 0:
                    minus_T(t, c + 1)
                else:
                    products(t, c - 1, 1, 2 if b + 1 < B else None, lambda: minus_T(t, c + 1))
                scores_T(t, c, 1)
                if b + 2 < B:
                    scores(t, c + 2, 0)
                if b >= 1:
                    out_T(t, c - 1)

                def between():
                    if b >= 1:
                        out_proj(t, c - 1)
                    if b + 2 < B:
                        scores(t, c + 2, 1)
                if b == B - 2:
                    gate_products(0, CB).then_inc(lg_mm, 1)
                products(t, c, 0, 5, between)
                if b >= 2:
                    turn_x(t, c - 2, 2)
            attention_steps(step)(pe)

            def first(k):
                ch, e = divmod(k, E)
                pe.wait_ge(w1_done, e + 1)
                after(pe, gelu_done, k - 1)
                a = slice(N * ch, N * (ch + 1))
                for fh in range(FH):
                    w = slice(P * fh, P * fh + P)
                    for i, (l, r) in enumerate(((w1_lo, xf_hi), (w1_hi, xf_lo), (w1_hi, xf_hi))):
                        last = nc.tensor.matmul(ps[:, 2 * (k % 2) + fh, :], l[:, e, w], r[:, a],
                                                start=(i == 0), stop=(i == 2))
                last.then_inc(f1_done, 1)

            def second(k):
                ch, e = divmod(k, E)
                u = k % 2
                pe.wait_ge(w2_done, e + 1)
                pe.wait_ge(hlo_done, k + 1)
                after(pe, yw_done, k - 1)
                for fh in range(FH):
                    for i, (l, r) in enumerate(((w2_hi, h_hi), (w2_lo, h_hi), (w2_hi, h_lo))):
                        last = nc.tensor.matmul(ps[:, 4 + u, :], l[:, e, fh, :], r[u][:, fh, :],
                                                start=(fh == 0 and i == 0), stop=(fh == FH - 1 and i == 2))
                last.then_inc(f2_done, 1)

            def out_turn(ch, y, start, stop):
                for i in range(CB):
                    last = nc.tensor.matmul(ps_y[:, D * i:D * i + D], y[:, S * i:S * i + S], id_sb,
                                            start=start and i == 0, stop=stop and i == CB - 1)
                if stop:
                    last.then_inc(y_done, 1)

            last = B // 2 - 1
            products(last, 1, 1)
            comb_turn(0)
            pe.wait_ge(max_done, 2 * B)
            pe.wait_ge(xlo_done, CB)
            first(0)
            pe.wait_ge(xT_sb, B - 2)
            out_T(last, 1)
            pe.wait_ge(cT_sb, 1)
            gate_products(CB, B - 2)
            out_proj(last, 1)
            first(1)
            turn_x(last, 0, 2)
            first(2)
            pe.wait_ge(on_done, B)
            for k in range(UNITS):
                second(k)
                if k == 0:
                    pe.wait_ge(xT_sb, B - 1)
                    turn_x(last, 1, 1)
                if k == 1:
                    gate_products(B - 2, B).then_inc(lg_mm, 1)
                if k == 6:
                    comb_turn(1)
                if k + 3 == E:
                    pe.wait_ge(xlo_done, B)
                if k + 3 < UNITS:
                    first(k + 3)
                if k == E + 1:
                    pe.wait_ge(yT_done, E)
                    out_turn(0, y_T[:, 0, :], True, True)
                if k == UNITS - 2:
                    pe.wait_ge(yT_done, UNITS - 2)
                    pe.wait_ge(acc_done, 2)
                    out_turn(1, y_T[:, 1, :], True, False)
            pe.wait_ge(yw_done, UNITS - 1)
            out_turn(1, y_w[0], False, False)
            pe.wait_ge(yw_done, UNITS)
            out_turn(1, y_w[1], False, True)


def kernel(**inputs):
    import numpy as np
    import concourse.bacc as bacc
    from concourse.bass_utils import run_bass_kernel_spmd as run

    a = {k: np.asarray(v) for k, v in inputs.items()}
    head_major = lambda w: w.reshape(w.shape[0], G, 2, DK).transpose(0, 2, 3, 1).reshape(w.shape[0], D)
    arrays = {
        "x": a["x"],
        "ctxT": a["ctx_1024"].reshape(B * S, D).T,
        "pack_k": np.concatenate([head_major(a["L0_xattn_Wk"]), head_major(a["L0_xattn_Wq"]),
                                  np.eye(P, dtype=np.float32), head_major(a["L0_xattn_bk"][None, :]).T,
                                  head_major(a["L0_xattn_bq"][None, :]).T, a["L0_ffn_ln_gamma"][:, None],
                                  a["L0_ffn_ln_beta"][:, None], a["L0_ffn_gate_w"].T], axis=1),
        "pack_v": np.concatenate([a["L0_xattn_Wv"], a["L0_xattn_Wo"]], axis=1),
        "row": np.concatenate([a["L0_xattn_bv"], a["L0_xattn_bo"],
                               np.tril(np.ones((E, E), np.float32), -1).reshape(-1)])[None, :],
        "w1T": a["L0_ffn_w1"].transpose(0, 2, 1),
        "w2T": a["L0_ffn_w2"].transpose(0, 2, 1).reshape(E, FH, P, D).transpose(0, 2, 1, 3),
    }
    arrays = {k: np.ascontiguousarray(v) for k, v in arrays.items()}
    nc = bacc.Bacc("TRN2", target_bir_lowering=False, num_devices=1)
    args = {k: nc.dram_tensor(f"in_{k}", v.shape, mybir.dt.from_np(v.dtype), kind="ExternalInput").ap()
            for k, v in arrays.items()}
    comb_d = nc.dram_tensor("comb_T_dram", (CH, CB * E, S), F32, kind="Internal").ap()
    out = nc.dram_tensor("out", (B, S, D), F32, kind="ExternalOutput").ap()
    build(nc, comb_d=comb_d, out=out, **args)
    r = run(nc, [{f"in_{k}": v for k, v in arrays.items()}], core_ids=[0])
    return r.results[0]["out"]
```
